# Optimizing a Trainium2 kernel written in Bass

```python
import numpy as np
import jax
import jax.numpy as jnp

def _softmax(x, axis=-1):
    return jax.nn.softmax(x, axis=axis)

def _gelu(x):
    return jax.nn.gelu(x, approximate=True)

def _silu(x):
    return jax.nn.silu(x)

def _sigmoid(x):
    return jax.nn.sigmoid(x)

def _layernorm(x, axis=-1, eps=1e-05):
    m = jnp.mean(x, axis=axis, keepdims=True)
    v = jnp.var(x, axis=axis, keepdims=True)
    return (x - m) / jnp.sqrt(v + eps)

def _scatter_add(tgt, idx, src, axis=0):
    return tgt.at[idx].add(src)

def _segment_sum(src, seg, n):
    return jax.ops.segment_sum(src, seg, n)
kernel_name = 'mk_adj_preln_d2_adj_r2_c9d73a'

def setup_inputs(seed: int=0):
    np.random.seed(seed)
    _w = jnp.asarray

    def _rec_inputs():
        import jax
        import jax.numpy as jnp
        _gk = jax.random.key(seed)
        x = -0.0001538 + 1 * jax.random.normal(jax.random.fold_in(_gk, 1), (8, 1024, 384), jnp.float32)
        _a = jax.random.bernoulli(jax.random.fold_in(_gk, 2), 0.0078125, (8, 1024, 1024))
        _a = jnp.logical_or(_a, jnp.swapaxes(_a, -1, -2))
        _a = jnp.logical_or(_a, jnp.eye(1024, dtype=bool))
        _af = _a.astype(jnp.float32)
        _af = _af * jax.random.uniform(jax.random.fold_in(_gk, 3), (8, 1024, 1024), jnp.float32, 0.05, 0.999992)
        adj = _af
        return (x, adj)
    x, adj = _rec_inputs()

    def _L0_gnn_setup():
        import jax, jax.numpy as jnp
        import numpy as np
        B, N, D, H = (8, 512, 384, 12)
        HD = D // H

        def _split_heads(x):
            b, n, _ = x.shape
            return x.reshape(b, n, H, HD).transpose(0, 2, 1, 3)
        key = jax.random.key(seed)
        ks = jax.random.split(key, 10)
        input_graph = jax.random.normal(ks[0], (B, N, D), dtype=jnp.float32)
        u = jax.random.uniform(ks[1], (B, N, N), dtype=jnp.float32)
        keep = jax.random.uniform(ks[2], (B, N, N)) < 0.15
        adj = jnp.where(keep, u, 0.0)
        s = 1.0 / np.sqrt(D)
        Wq = jax.random.normal(ks[3], (D, D), dtype=jnp.float32) * s
        bq = jnp.zeros((D,), dtype=jnp.float32)
        Wk = jax.random.normal(ks[4], (D, D), dtype=jnp.float32) * s
        bk = jnp.zeros((D,), dtype=jnp.float32)
        Wv = jax.random.normal(ks[5], (D, D), dtype=jnp.float32) * s
        bv = jnp.zeros((D,), dtype=jnp.float32)
        beta = jnp.asarray(0.1, dtype=jnp.float32)
        return {'input_graph': input_graph, 'adj': adj, 'Wq': Wq, 'bq': bq, 'Wk': Wk, 'bk': bk, 'Wv': Wv, 'bv': bv, 'beta': beta}
    _L0_gnn_all = _L0_gnn_setup()
    _L0_gnn_in = {k: v for k, v in _L0_gnn_all.items() if k in ('Wq', 'bq', 'Wk', 'bk', 'Wv', 'bv', 'beta')}
    del _L0_gnn_all

    def _L1_gnn_setup():
        import jax, jax.numpy as jnp
        import numpy as np
        NUM_HEADS = 12
        HIDDEN = 384
        HEAD = HIDDEN // NUM_HEADS
        SCALE = HIDDEN ** (-0.5)
        key = jax.random.key(seed)
        ks = jax.random.split(key, 8)
        B, N = (16, 256)
        std = HIDDEN ** (-0.5)
        return {'x': jax.random.normal(ks[0], (B, N, HIDDEN), dtype=jnp.float32), 'encoding_bias': jax.random.normal(ks[1], (B, N, N), dtype=jnp.float32), 'Wq': jax.random.normal(ks[2], (HIDDEN, HIDDEN), dtype=jnp.float32) * std, 'Wk': jax.random.normal(ks[3], (HIDDEN, HIDDEN), dtype=jnp.float32) * std, 'Wv': jax.random.normal(ks[4], (HIDDEN, HIDDEN), dtype=jnp.float32) * std, 'bv': jax.random.normal(ks[5], (HIDDEN,), dtype=jnp.float32) * 0.01, 'Wo': jax.random.normal(ks[6], (HIDDEN, HIDDEN), dtype=jnp.float32) * std, 'bo': jax.random.normal(ks[7], (HIDDEN,), dtype=jnp.float32) * 0.01}
    _L1_gnn_all = _L1_gnn_setup()
    _L1_gnn_in = {k: v for k, v in _L1_gnn_all.items() if k in ('Wq', 'Wk', 'Wv', 'bv', 'Wo', 'bo')}
    del _L1_gnn_all
    return {'x': x, 'adj': adj, 'L0_gnn_Wq': _L0_gnn_in['Wq'], 'L0_gnn_bq': _L0_gnn_in['bq'], 'L0_gnn_Wk': _L0_gnn_in['Wk'], 'L0_gnn_bk': _L0_gnn_in['bk'], 'L0_gnn_Wv': _L0_gnn_in['Wv'], 'L0_gnn_bv': _L0_gnn_in['bv'], 'L0_gnn_beta': _L0_gnn_in['beta'], 'L1_gnn_Wq': _L1_gnn_in['Wq'], 'L1_gnn_Wk': _L1_gnn_in['Wk'], 'L1_gnn_Wv': _L1_gnn_in['Wv'], 'L1_gnn_bv': _L1_gnn_in['bv'], 'L1_gnn_Wo': _L1_gnn_in['Wo'], 'L1_gnn_bo': _L1_gnn_in['bo']}

def reference(x, adj, L0_gnn_Wq, L0_gnn_bq, L0_gnn_Wk, L0_gnn_bk, L0_gnn_Wv, L0_gnn_bv, L0_gnn_beta, L1_gnn_Wq, L1_gnn_Wk, L1_gnn_Wv, L1_gnn_bv, L1_gnn_Wo, L1_gnn_bo):
    import jax
    import jax.numpy as jnp

    def _L0_gnn_ref(input_graph, adj, Wq, bq, Wk, bk, Wv, bv, beta):
        import jax, jax.numpy as jnp
        import numpy as np
        B, N, D, H = (8, 512, 384, 12)
        HD = D // H

        def _split_heads(x):
            b, n, _ = x.shape
            return x.reshape(b, n, H, HD).transpose(0, 2, 1, 3)
        q = _split_heads(input_graph @ Wq + bq)
        k = _split_heads(input_graph @ Wk + bk)
        v = _split_heads(input_graph @ Wv + bv)
        scores = jnp.einsum('bhqd,bhkd->bhqk', q, k) / jnp.sqrt(jnp.asarray(HD, input_graph.dtype))
        adj_e = adj[:, None, :, :]
        scores = scores + beta * adj_e
        scores = jnp.where(adj_e > 0, scores, jnp.asarray(-9000000000000000.0, scores.dtype))
        probs = jax.nn.softmax(scores, axis=-1)
        out = jnp.einsum('bhqk,bhkd->bhqd', probs, v)
        return out.transpose(0, 2, 1, 3).reshape(input_graph.shape[0], input_graph.shape[1], D)

    def _L1_gnn_ref(x, encoding_bias, Wq, Wk, Wv, bv, Wo, bo):
        import jax, jax.numpy as jnp
        import numpy as np
        NUM_HEADS = 12
        HIDDEN = 384
        HEAD = HIDDEN // NUM_HEADS
        SCALE = HIDDEN ** (-0.5)
        B, N, _ = x.shape
        q = (x @ Wq.T).reshape(B, N, NUM_HEADS, HEAD)
        k = (x @ Wk.T).reshape(B, N, NUM_HEADS, HEAD)
        v = (x @ Wv.T + bv).reshape(B, N, NUM_HEADS, HEAD)
        a = jnp.einsum('bnhd,bmhd->bhnm', q, k) * SCALE + encoding_bias[:, None, :, :]
        pad_mask = jnp.all(a == 0, axis=-1)
        a = jnp.where(pad_mask[..., None], -jnp.inf, a)
        a = jax.nn.softmax(a, axis=-1)
        a = jnp.nan_to_num(a)
        o = jnp.einsum('bhnm,bmhd->bnhd', a, v).reshape(B, N, HIDDEN)
        return o @ Wo.T + bo
    h = jnp.maximum(_layernorm(x, axis=-1), 0.0)
    x = x + _L0_gnn_ref(h, adj, L0_gnn_Wq, L0_gnn_bq, L0_gnn_Wk, L0_gnn_bk, L0_gnn_Wv, L0_gnn_bv, L0_gnn_beta)
    h = jnp.maximum(_layernorm(x, axis=-1), 0.0)
    x = x + _L1_gnn_ref(h, adj, L1_gnn_Wq, L1_gnn_Wk, L1_gnn_Wv, L1_gnn_bv, L1_gnn_Wo, L1_gnn_bo)
    return x

_drawn_inputs = setup_inputs


def setup_inputs(seed=0):
    import zlib

    import numpy as np

    out = dict(_drawn_inputs(seed))
    spreads = {'L0_gnn_bq': (0.0, 0.8), 'L0_gnn_bk': (0.0, 0.8), 'L0_gnn_bv': (0.0, 0.1)}
    factors = {'L1_gnn_Wq': 8.0, 'L1_gnn_Wk': 8.0, 'L1_gnn_bv': 5.96, 'L1_gnn_bo': 6.578}
    for name, (base, spread) in spreads.items():
        noise = np.random.default_rng([zlib.crc32(name.encode()), seed]).standard_normal(out[name].shape)
        drawn = base * np.exp(spread * noise) if base else spread * noise
        out[name] = jnp.asarray(drawn.astype(out[name].dtype))
    for name, factor in factors.items():
        out[name] = (out[name] * factor).astype(out[name].dtype)
    return out
```

```python
from contextlib import ExitStack

import concourse.bass as bass
from concourse import mybir

F32 = mybir.dt.float32
F32R = mybir.dt.float32r
ALU = mybir.AluOpType
ACT = mybir.ActivationFunctionType

P = 128
B, N, D, H = 8, 1024, 384, 12
HD = D // H
NT = N // P
KD = D // P
HG = P // HD
HALF = 512
GROUPS = B * KD
CHUNK = 256
CHUNKS = N // CHUNK
QT = CHUNK // P
TILES = CHUNKS * HG * QT
CT = HG * QT
LATE = 2
SLOTS = GROUPS * CHUNKS + LATE
EPS = 1e-5
MASKED = -9.0e15
BIG = 3.0e38
GONE = -1.0e30
TINY = 1.0e-30


class Scratch:

    def __init__(self, nc):
        self.q = nc.dram_tensor("q_parts", [GROUPS, 2, P, N], F32).ap()
        self.k = nc.dram_tensor("k_parts", [GROUPS, 2, P, N], F32).ap()
        self.v = nc.dram_tensor("v_rows", [GROUPS, P, NT * P], F32).ap()
        self.o = nc.dram_tensor("attended_t", [SLOTS, P, CHUNK], F32).ap()
        self.x1 = nc.dram_tensor("x_between", [B, N, D], F32).ap()


class Mem:

    def __init__(self, nc, ctx, tag):
        self.nc, self.ctx, self.tag = nc, ctx, tag
        self.holds = self.sem("holds")

    def hold(self, eng, sem, value):
        eng.wait_ge(sem, value)
        eng.sem_inc(self.holds, 1)

    def sb(self, name, shape, dt=F32):
        return self.ctx.enter_context(self.nc.sbuf_tensor(f"{name}_{self.tag}", shape, dt))

    def ps(self, name, shape):
        return self.ctx.enter_context(self.nc.psum_tensor(f"{name}_{self.tag}", shape, F32))

    def sem(self, name):
        return self.ctx.enter_context(self.nc.semaphore(f"{name}_{self.tag}"))


def project(nc, layer, x_in, ident_in, wq_in, wk_in, wv_in, bq_in, bk_in, bv_in, scratch):
    q_scale = float(HD) ** -0.5 if layer == 0 else float(D) ** -0.5
    UNITS = 2 * KD * 2
    with ExitStack() as ctx:
        m = Mem(nc, ctx, f"project{layer}")
        ident = m.sb("ident", [P, P])
        w = m.sb("w", [P, 3, KD, D])
        qk_bias = m.sb("qk_bias", [P, 2, KD])
        v_bias = m.sb("v_bias", [P, D])
        x = m.sb("x", [P, NT, D])
        att = m.sb("att", [P, KD * CHUNKS, CHUNK])
        h = m.sb("h", [P, NT, D])
        stats = m.sb("stats", [P, NT, 6])
        moments = m.sb("moments", [P, NT, 2])
        var = m.sb("var", [P, NT])
        std = m.sb("std", [P, NT])
        rstd = m.sb("rstd", [P, NT])
        h_t = m.sb("h_t", [P, KD, N])
        full = m.sb("full", [P, 2, HALF])
        high = m.sb("high", [P, 2, HALF], F32R)
        low = m.sb("low", [P, 2, HALF], F32R)
        v_out = m.sb("v_out", [P, 2, D])
        turn_ps = m.ps("turn_ps", [P, 2, HALF])
        att_ps = m.ps("att_ps", [P, 2, HALF])
        qk_ps = m.ps("qk_ps", [P, 2, HALF])
        v_ps = m.ps("v_ps", [P, 2, HALF])

        consts_in = m.sem("consts_in")
        x_loaded = m.sem("x_loaded")
        att_loaded = m.sem("att_loaded")
        x_free = m.sem("x_free")
        att_turned = m.sem("att_turned")
        x_added = m.sem("x_added")
        x1_stored = m.sem("x1_stored")
        stats_done = m.sem("stats_done")
        moments_done = m.sem("moments_done")
        var_ready = m.sem("var_ready")
        std_ready = m.sem("std_ready")
        rstd_ready = m.sem("rstd_ready")
        h_ready = m.sem("h_ready")
        h_turned = m.sem("h_turned")
        h_t_ready = m.sem("h_t_ready")
        qk_done = m.sem("qk_done")
        full_ready = m.sem("full_ready")
        high_ready = m.sem("high_ready")
        low_ready = m.sem("low_ready")
        qk_stored = [m.sem(f"qk_stored{i}") for i in range(2)]
        v_done = m.sem("v_done")
        v_ready = m.sem("v_ready")
        v_stored = [m.sem(f"v_stored{i}") for i in range(2)]
        N_CONSTS = 4 + (3 if layer == 0 else 1)

        block = ctx.enter_context(nc.Block())

        @block.sync
        def _(sp):
            for t, src in enumerate((wq_in, wk_in, wv_in)):
                sp.dma_start(w[:, t], src.rearrange("(c p) n -> p c n", p=P)).then_inc(consts_in, 16)
            sp.dma_start(ident[:], ident_in).then_inc(consts_in, 16)
            sp.dma_start(v_bias[:], bv_in.partition_broadcast(P)).then_inc(consts_in, 16)
            if layer == 0:
                sp.dma_start(qk_bias[:, 0, :], bq_in).then_inc(consts_in, 16)
                sp.dma_start(qk_bias[:, 1, :], bk_in).then_inc(consts_in, 16)
            with sp.Fori(0, B) as b:
                if layer == 1:
                    m.hold(sp, x_added, (b + 1) * NT)
                    sp.dma_start(scratch.x1[bass.ds(b, 1)].rearrange("a (t p) d -> p (a t) d", p=P), x[:]).then_inc(x1_stored, 16)
                for u in range(UNITS):
                    tensor, fg, half = u // (2 * KD), u // 2 % KD, u % 2
                    dst = (scratch.q, scratch.k)[tensor]
                    for part, tile, ready in ((0, high, high_ready), (1, low, low_ready)):
                        m.hold(sp, ready, b * UNITS + u + 1)
                        sp.dma_start(dst[bass.ds(b * KD + fg, 1), part, :, half * HALF:(half + 1) * HALF].rearrange("a p n -> (a p) n"),
                                     tile[:, u % 2].bitcast(F32)).then_inc(qk_stored[u % 2], 16)
                for t in range(NT):
                    m.hold(sp, v_ready, b * NT + t + 1)
                    sp.dma_start(scratch.v[bass.ds(b * KD, KD), :, t * P:(t + 1) * P].rearrange("g p f -> p g f"),
                                 v_out[:, t % 2].rearrange("p (g f) -> p g f", g=KD)).then_inc(v_stored[t % 2], 16)
            for i in range(2):
                sp.wait_ge(qk_stored[i], 32 * (UNITS // 2 * B + 1))
                sp.wait_ge(v_stored[i], 16 * (NT // 2 * B + 1))
            if layer == 1:
                sp.wait_ge(x1_stored, 16 * (B + 1))

        @block.gpsimd
        def _(pool):
            pool.nop().then_inc(x_free, NT)
            for i in range(2):
                pool.nop().then_inc(qk_stored[i], 32)
                pool.nop().then_inc(v_stored[i], 16)
            if layer == 1:
                pool.nop().then_inc(x1_stored, 16)
            with pool.Fori(0, B) as b:
                pool.wait_ge(x_free, NT * (b + 1))
                if layer == 1:
                    pool.wait_ge(x1_stored, 16 * (b + 1))
                pool.dma_start(x[:], x_in[bass.ds(b, 1)].rearrange("a (t p) d -> p (a t) d", p=P)).then_inc(x_loaded, 16)
                if layer == 1:
                    pool.dma_start(att[:], scratch.o[bass.ds(b * (KD * CHUNKS) + LATE, KD * CHUNKS)].rearrange("s p n -> p s n")).then_inc(att_loaded, 16)

        @block.scalar
        def _(act):
            with act.Fori(0, B) as b:
                act.wait_ge(var_ready, b + 1)
                nc.scalar.activation(std[:], var[:], ACT.Sqrt).then_inc(std_ready, 1)
                for t in range(NT):
                    act.wait_ge(h_turned, b * NT + t + 1)
                    nc.scalar.activation(h_t[:, :, t * P:(t + 1) * P], turn_ps[:, t % 2, 0:D].rearrange("p (c n) -> p c n", c=KD),
                                         ACT.Relu).then_inc(h_t_ready, 1)
                for u in range(UNITS):
                    act.wait_ge(full_ready, b * UNITS + u + 1)
                    act.wait_ge(qk_stored[u % 2], 32 * (b * (UNITS // 2) + u // 2 + 1))
                    nc.scalar.activation(high[:, u % 2], full[:, u % 2], ACT.Copy).then_inc(high_ready, 1)

        @block.vector
        def _(dve):
            dve.wait_ge(consts_in, 16 * N_CONSTS)
            with dve.Fori(0, B) as b:
                dve.wait_ge(x_loaded, 16 * (b + 1))
                if layer == 1:
                    for t in range(NT):
                        dve.wait_ge(att_turned, b * NT + t + 1)
                        nc.vector.tensor_tensor(x[:, t], x[:, t], att_ps[:, t % 2, 0:D], ALU.add).then_inc(x_added, 1)
                for t in range(NT):
                    if layer == 1:
                        dve.wait_ge(x_added, b * NT + t + 1)
                    nc.vector.bn_stats(stats[:, t], x[:, t]).then_inc(stats_done, 1)
                for t in range(NT):
                    m.hold(dve, stats_done, b * NT + t + 1)
                    nc.vector.bn_aggr(moments[:, t], stats[:, t]).then_inc(moments_done, 1)
                dve.wait_ge(moments_done, (b + 1) * NT)
                nc.vector.tensor_scalar(var[:], moments[:, :, 1], EPS, None, ALU.add).then_inc(var_ready, 1)
                dve.wait_ge(std_ready, b + 1)
                nc.vector.reciprocal(rstd[:], std[:]).then_inc(rstd_ready, 1)
                dve.wait_ge(rstd_ready, b + 1)
                for t in range(NT):
                    nc.vector.tensor_scalar(h[:, t], x[:, t], moments[:, t, 0:1], rstd[:, t:t + 1], ALU.subtract, ALU.mult).then_inc(h_ready, 1)
                dve.wait_ge(h_ready, (b + 1) * NT)
                dve.nop().then_inc(x_free, NT)
                for u in range(UNITS):
                    tensor, fg = u // (2 * KD), u // 2 % KD
                    dve.wait_ge(qk_done, b * UNITS + u + 1)
                    dve.wait_ge(qk_stored[u % 2], 32 * (b * (UNITS // 2) + u // 2 + 1))
                    bias = qk_bias[:, tensor, fg:fg + 1] if layer == 0 else 0.0
                    nc.vector.tensor_scalar(full[:, u % 2], qk_ps[:, u % 2], bias, 1.0 if tensor else q_scale,
                                            ALU.add, ALU.mult).then_inc(full_ready, 1)
                    dve.wait_ge(high_ready, b * UNITS + u + 1)
                    nc.vector.tensor_tensor(low[:, u % 2], full[:, u % 2], high[:, u % 2].bitcast(F32), ALU.subtract).then_inc(low_ready, 1)
                for t in range(NT):
                    dve.wait_ge(v_done, b * NT + t + 1)
                    dve.wait_ge(v_stored[t % 2], 16 * (b * (NT // 2) + t // 2 + 1))
                    nc.vector.tensor_tensor(v_out[:, t % 2], v_ps[:, t % 2, 0:D], v_bias[:], ALU.add).then_inc(v_ready, 1)

        @block.tensor
        def _(pe):
            pe.wait_ge(consts_in, 16 * N_CONSTS)
            with pe.Fori(0, B) as b:
                if layer == 1:
                    pe.wait_ge(att_loaded, 16 * (b + 1))
                    for t in range(NT):
                        if t >= 2:
                            pe.wait_ge(x_added, b * NT + t - 1)
                        for g in range(KD):
                            last = nc.tensor.transpose(att_ps[:, t % 2, g * P:(g + 1) * P],
                                                       att[:, g * CHUNKS + t // QT, (t % QT) * P:(t % QT + 1) * P], ident[:])
                        last.then_inc(att_turned, 1)
                for t in range(NT):
                    pe.wait_ge(h_ready, b * NT + t + 1)
                    if t >= 2:
                        pe.wait_ge(h_t_ready, b * NT + t - 1)
                    for c in range(KD):
                        last = nc.tensor.transpose(turn_ps[:, t % 2, c * P:(c + 1) * P], h[:, t, c * P:(c + 1) * P], ident[:])
                    last.then_inc(h_turned, 1)
                pe.wait_ge(h_t_ready, (b + 1) * NT)
                for u in range(UNITS):
                    tensor, fg, half = u // (2 * KD), u // 2 % KD, u % 2
                    if u >= 2:
                        pe.wait_ge(full_ready, b * UNITS + u - 1)
                    for c in range(KD):
                        last = nc.tensor.matmul(qk_ps[:, u % 2], w[:, tensor, c, fg * P:(fg + 1) * P],
                                                h_t[:, c, half * HALF:(half + 1) * HALF], start=(c == 0), stop=(c == KD - 1))
                    last.then_inc(qk_done, 1)
                for t in range(NT):
                    if t >= 2:
                        pe.wait_ge(v_ready, b * NT + t - 1)
                    for c in range(KD):
                        last = nc.tensor.matmul(v_ps[:, t % 2, 0:D], h_t[:, c, t * P:(t + 1) * P], w[:, 2, c, :],
                                                start=(c == 0), stop=(c == KD - 1))
                    last.then_inc(v_done, 1)


def attend(nc, layer, adj_in, ident_in, beta_in, scratch):
    with ExitStack() as ctx:
        m = Mem(nc, ctx, f"attend{layer}")
        ident = m.sb("ident", [P, P])
        ones = m.sb("ones", [P, HD])
        beta = m.sb("beta", [P, 1])
        q_st = m.sb("q_st", [P, HG, N], F32R)
        k_st = m.sb("k_st", [P, HG, N], F32R)
        v_now = m.sb("v_now", [P, NT, P])
        v_kept = m.sb("v_kept", [P, NT, P])
        bias = m.sb("bias", [P, NT, N])
        neg = m.sb("neg", [P, 4, N])
        shifted = m.sb("shifted", [P, 4, N])
        neg_max = m.sb("neg_max", [P, TILES])
        if layer == 0:
            adj = m.sb("adj", [P, QT, N])
            masked = m.sb("masked", [P, N])
            shift = neg_max
        else:
            spare = m.sb("spare", [P, N])
            neg_min = m.sb("neg_min", [P, TILES])
            max_zero = m.sb("max_zero", [P, TILES])
            all_zero = m.sb("all_zero", [P, TILES])
            shift = m.sb("shift", [P, TILES])
        probs = m.sb("probs", [P, 2, HG, NT, CHUNK])
        sums_inv = m.sb("sums_inv", [P, 2, CHUNK])
        out_t = m.sb("out_t", [P, 2, CHUNK])
        s_ps = m.ps("s_ps", [P, 2, N])
        t_ps = m.ps("t_ps", [P, 2, HALF])
        o_ps = m.ps("o_ps", [P, 2, HALF])

        consts_in = m.sem("consts_in")
        inited = m.sem("inited")
        qk_loaded = [m.sem(f"qk_loaded{j}") for j in range(HG)]
        adj_loaded = [m.sem(f"adj_loaded{c}") for c in range(CHUNKS)]
        v_loaded = m.sem("v_loaded")
        v_copied = m.sem("v_copied")
        scored = m.sem("scored")
        negated = m.sem("negated")
        checked = m.sem("checked")
        max_zero_ready = m.sem("max_zero_ready")
        all_zero_ready = m.sem("all_zero_ready")
        shift_ready = m.sem("shift_ready") if layer else negated
        score_read = checked if layer else negated
        shifted_ready = m.sem("shifted_ready")
        turned = m.sem("turned")
        exp_done = m.sem("exp_done")
        pv_done = m.sem("pv_done")
        masked_ready = m.sem("masked_ready")
        weighted = m.sem("weighted")
        bias_ready = m.sem("bias_ready")
        adj_used = m.sem("adj_used")
        sums_ready = m.sem("sums_ready")
        inv_ready = m.sem("inv_ready")
        out_ready = m.sem("out_ready")
        out_stored = [m.sem(f"out_stored{i}") for i in range(2)]
        QK_IN = 16 * 8

        block = ctx.enter_context(nc.Block())

        @block.sync
        def _(sp):
            def load_qk(r, j):
                heads = slice(j * HD, (j + 1) * HD)
                for row, part in enumerate((0, 0, 1, 1)):
                    sp.dma_start(q_st[row * HD:(row + 1) * HD, j].bitcast(F32),
                                 scratch.q[bass.ds(r, 1), part, heads, :].rearrange("a p n -> (a p) n")).then_inc(qk_loaded[j], 16)
                for row, part in enumerate((0, 1, 0, 1)):
                    sp.dma_start(k_st[row * HD:(row + 1) * HD, j].bitcast(F32),
                                 scratch.k[bass.ds(r, 1), part, heads, :].rearrange("a p n -> (a p) n")).then_inc(qk_loaded[j], 16)

            def load_adj(b, c):
                dst = adj[:] if layer == 0 else bias[:, c * QT:(c + 1) * QT]
                sp.dma_start(dst, adj_in[bass.ds(b, 1), c * CHUNK:(c + 1) * CHUNK, :].rearrange("a (t p) n -> p (a t) n", p=P)).then_inc(adj_loaded[c], 16)

            def load_v(r):
                sp.dma_start(v_now[:], scratch.v[bass.ds(r, 1)].rearrange("a p (t f) -> (a p) t f", t=NT)).then_inc(v_loaded, 16)

            def store(n, i):
                m.hold(sp, out_ready, n + 2)
                sp.dma_start(scratch.o[bass.ds(n, 1)].rearrange("a p n -> (a p) n"), out_t[:, i]).then_inc(out_stored[i], 16)

            def group(r, next_r, refill):
                for c in range(CHUNKS):
                    if c == CHUNKS - 1:
                        for j in range(HG // 2):
                            m.hold(sp, scored, r * TILES + c * CT + (j + 1) * QT)
                            load_qk(next_r, j)
                    store(r * CHUNKS + c, c % 2)
                    if c == CHUNKS - 1:
                        for j in range(HG // 2, HG):
                            m.hold(sp, scored, r * TILES + c * CT + (j + 1) * QT)
                            load_qk(next_r, j)
                    if refill is not None:
                        this_b, next_b = refill
                        if layer == 0:
                            m.hold(sp, adj_used, (this_b + 1) * CHUNKS + c)
                        else:
                            m.hold(sp, score_read, r * TILES + (c + 1) * CT + layer)
                        load_adj(next_b, c)
                m.hold(sp, pv_done, r * CHUNKS + CHUNKS - 2 + LATE + 1)
                m.hold(sp, v_copied, r + 2)
                load_v(next_r)

            sp.dma_start(ident[:], ident_in).then_inc(consts_in, 16)
            sp.dma_start(beta[:], beta_in.partition_broadcast(P)).then_inc(consts_in, 16)
            for c in range(CHUNKS):
                if c == 1:
                    for j in range(HG):
                        load_qk(0, j)
                    load_v(0)
                if layer == 0 and c:
                    m.hold(sp, adj_used, c)
                load_adj(0, c)
            with sp.Fori(0, B - 1) as b:
                with sp.Fori(0, KD - 1) as g:
                    group(b * KD + g, b * KD + g + 1, None)
                group(b * KD + KD - 1, b * KD + KD, (b, b + 1))
            for r in range(GROUPS - KD, GROUPS):
                group(r, min(r + 1, GROUPS - 1), (B - 1, B - 1) if r == GROUPS - 1 else None)
            for i in range(LATE):
                store(GROUPS * CHUNKS + i, i)
            for i in range(2):
                sp.wait_ge(out_stored[i], 16 * (SLOTS // 2 + 1))
            for j in range(HG):
                sp.wait_ge(qk_loaded[j], QK_IN * (GROUPS + 1))
            for c in range(CHUNKS):
                sp.wait_ge(adj_loaded[c], 16 * (B + 1))
            sp.wait_ge(v_loaded, 16 * (GROUPS + 1))

        @block.gpsimd
        def _(pool):
            nc.gpsimd.memset(probs[:, 0, :, 0], 1.0).then_inc(inited, 1)
            nc.gpsimd.memset(v_kept[:], 0.0).then_inc(inited, 1)
            nc.gpsimd.memset(ones[:], 1.0).then_inc(inited, 1)
            nc.gpsimd.memset(probs[:, 1], 1.0).then_inc(inited, 1)
            with pool.Fori(0, GROUPS) as r:
                for t in range(TILES):
                    m.hold(pool, shift_ready, r * TILES + t + 1)
                    nc.gpsimd.tensor_scalar(shifted[:, t % 4], neg[:, t % 4], -1.0, shift[:, t:t + 1],
                                            ALU.mult, ALU.add).then_inc(shifted_ready, 1)

        @block.scalar
        def _(act):
            act.nop().then_inc(exp_done, 2)
            for i in range(2):
                act.nop().then_inc(out_stored[i], 16)
            with act.Fori(0, GROUPS) as r:
                for t in range(TILES):
                    c, j, u = t // CT, t // QT % HG, t % QT
                    if t % CT == 0:
                        act.wait_ge(pv_done, r * CHUNKS + c - 2 + LATE + 1)
                    for half in range(2):
                        keys = slice(half * NT // 2, (half + 1) * NT // 2)
                        act.wait_ge(turned, (r * TILES + t) * 2 + half + 1)
                        nc.scalar.activation(probs[:, c % 2, j, keys, u * P:(u + 1) * P],
                                             t_ps[:, half].rearrange("p (k n) -> p k n", k=NT // 2), ACT.Exp).then_inc(exp_done, 1)

        @block.vector
        def _(dve):
            def make_bias(b, c):
                dve.wait_ge(adj_loaded[c], 16 * (b + 1))
                for u in range(QT):
                    n = (b * CHUNKS + c) * QT + u
                    dve.wait_ge(bias_ready, n + 1)
                    nc.vector.tensor_scalar(masked[:], adj[:, u], 0.0, MASKED, ALU.is_le, ALU.mult).then_inc(masked_ready, 1)
                    dve.wait_ge(masked_ready, n + 1)
                    nc.vector.tensor_scalar(adj[:, u], adj[:, u], 0.0, beta[:, 0:1], ALU.max, ALU.mult).then_inc(weighted, 1)
                    dve.wait_ge(weighted, n + 1)
                    nc.vector.tensor_tensor(bias[:, c * QT + u], adj[:, u], masked[:], ALU.add).then_inc(bias_ready, 1)
                dve.wait_ge(bias_ready, (b * CHUNKS + c + 1) * QT + 1)
                dve.nop().then_inc(adj_used, 1)

            def finish(n, n_half, i):
                dve.wait_ge(pv_done, n + 1)
                nc.vector.reciprocal(sums_inv[:, i], o_ps[:, i, CHUNK:]).then_inc(inv_ready, 1)
                dve.wait_ge(inv_ready, n + 1)
                dve.wait_ge(out_stored[i], 16 * (n_half + 1))
                nc.vector.tensor_tensor(out_t[:, i], o_ps[:, i, 0:CHUNK], sums_inv[:, i], ALU.mult).then_inc(out_ready, 1)

            def group(b, r, refill_b):
                for t in range(TILES):
                    c, qi = t // CT, t // CT * QT + t % QT
                    n = r * TILES + t
                    if layer == 1 and t % CT == 0:
                        dve.wait_ge(adj_loaded[c], 16 * (b + 1))
                    m.hold(dve, scored, n + 1)
                    nc.vector.tensor_tensor_reduce(out=neg[:, t % 4], in0=s_ps[:, t % 2], in1=bias[:, qi], scale=-1.0, scalar=BIG,
                                                   op0=ALU.add, op1=ALU.min, accum_out=neg_max[:, t:t + 1]).then_inc(negated, 1)
                    if layer == 1:
                        dve.wait_ge(negated, n + 1)
                        m.hold(dve, checked, n + 1)
                        nc.vector.tensor_tensor_reduce(out=spare[:], in0=s_ps[:, t % 2], in1=bias[:, qi], scale=-1.0, scalar=-BIG,
                                                       op0=ALU.add, op1=ALU.max, accum_out=neg_min[:, t:t + 1]).then_inc(checked, 1)
                        nc.vector.tensor_scalar(max_zero[:, t:t + 1], neg_max[:, t:t + 1], 0.0, GONE, ALU.is_equal, ALU.mult).then_inc(max_zero_ready, 1)
                        dve.wait_ge(checked, n + 2)
                        dve.wait_ge(max_zero_ready, n + 1)
                        nc.vector.scalar_tensor_tensor(all_zero[:, t:t + 1], neg_min[:, t:t + 1], 0.0, max_zero[:, t:t + 1],
                                                       ALU.is_equal, ALU.mult).then_inc(all_zero_ready, 1)
                        dve.wait_ge(all_zero_ready, n + 1)
                        nc.vector.tensor_tensor(shift[:, t:t + 1], all_zero[:, t:t + 1], neg_max[:, t:t + 1], ALU.add).then_inc(shift_ready, 1)
                    if t % CT == 3:
                        finish(r * CHUNKS + c, r * (CHUNKS // 2) + c // 2, c % 2)
                    if t == 2 * CT:
                        dve.wait_ge(v_loaded, 16 * (r + 1))
                        dve.wait_ge(pv_done, r * CHUNKS - 1 + LATE + 1)
                        nc.vector.tensor_copy(v_kept[:], v_now[:]).then_inc(v_copied, 1)
                    if refill_b is not None and layer == 0 and t % CT == CT - 1:
                        dve.wait_ge(negated, n + 1)
                        make_bias(refill_b, c)

            dve.nop().then_inc(bias_ready, 1)
            dve.nop().then_inc(out_ready, 1)
            dve.nop().then_inc(v_copied, 1)
            dve.nop().then_inc(checked, 1)
            dve.wait_ge(consts_in, 32)
            dve.wait_ge(inited, 4)
            if layer == 0:
                for c in range(CHUNKS):
                    make_bias(0, c)
            with dve.Fori(0, B) as b:
                with dve.Fori(0, KD - 1) as g:
                    group(b, b * KD + g, None)
                group(b, b * KD + KD - 1, b + 1)
            for i in range(LATE):
                n = GROUPS * CHUNKS + i
                finish(n, n // 2, i)

        @block.tensor
        def _(pe):
            def score(t, n):
                c, j, u = t // CT, t // QT % HG, t % QT
                queries = slice((c * QT + u) * P, (c * QT + u + 1) * P)
                for half in range(2):
                    last = nc.tensor.matmul(s_ps[:, t % 2, half * HALF:(half + 1) * HALF], q_st[:, j, queries],
                                            k_st[:, j, half * HALF:(half + 1) * HALF], start=True, stop=True)
                last.then_inc(scored, 1)

            def products(i, buf, v, kt, stop):
                for j in range(HG):
                    nc.tensor.matmul(o_ps[j * HD:(j + 1) * HD, i, 0:CHUNK], v[:, kt, j * HD:(j + 1) * HD],
                                     probs[:, buf, j, kt], start=(kt == 0), stop=stop, skip_group_check=True)
                for j in range(HG):
                    last = nc.tensor.matmul(o_ps[j * HD:(j + 1) * HD, i, CHUNK:], ones[:],
                                            probs[:, buf, j, kt], start=False, stop=stop, skip_group_check=True)
                return last

            pe.wait_ge(inited, 4)
            pe.wait_ge(consts_in, 32)
            products(0, 0, v_kept, 0, True).then_inc(pv_done, 1)
            for t in range(2):
                pe.wait_ge(qk_loaded[t // QT], QK_IN)
                score(t, t)
            with pe.Fori(0, GROUPS) as r:
                for t in range(TILES):
                    c = t // CT
                    n = r * TILES + t
                    ahead = t + 2
                    if ahead % TILES < CT and ahead % QT == 0:
                        pe.wait_ge(qk_loaded[ahead % TILES // QT], QK_IN * (r + 1 + ahead // TILES))
                    pe.wait_ge(score_read, n + 1 + layer)
                    score(ahead % TILES, n + 2)
                    pe.wait_ge(shifted_ready, n + 1)
                    for half in range(2):
                        pe.wait_ge(exp_done, n * 2 + half + 1)
                        for k in range(NT // 2):
                            kt = half * NT // 2 + k
                            last = nc.tensor.transpose(t_ps[:, half, k * P:(k + 1) * P], shifted[:, t % 4, kt * P:(kt + 1) * P], ident[:])
                        last.then_inc(turned, 1)
                    if t % CT == 0:
                        pe.wait_ge(exp_done, (r * CHUNKS + c) * CT * 2 + 2)
                        pe.wait_ge(out_ready, r * CHUNKS + c + 1)
                        if c == 0:
                            pe.wait_ge(v_copied, r + 1)
                        if c == 1:
                            pe.wait_ge(v_loaded, 16 * (r + 1))
                    kt = t % CT
                    last = products((c + 1) % 2, (c + 1) % 2, v_now if c else v_kept, kt, kt == NT - 1)
                    if kt == NT - 1:
                        last.then_inc(pv_done, 1)
            pe.wait_ge(exp_done, TILES * GROUPS * 2 + 2)
            pe.wait_ge(out_ready, GROUPS * CHUNKS + 1)
            pe.wait_ge(v_copied, GROUPS + 1)
            for kt in range(NT):
                last = products(1, 1, v_kept, kt, kt == NT - 1)
            last.then_inc(pv_done, 1)


def finish(nc, wo_in, bo_in, scratch, out):
    with ExitStack() as ctx:
        m = Mem(nc, ctx, "finish")
        w = m.sb("w", [P, KD, D])
        bo = m.sb("bo", [P, D])
        x = m.sb("x", [P, 2, NT, D])
        att = m.sb("att", [P, 2, KD * CHUNKS, CHUNK])
        y_ps = m.ps("y_ps", [P, 2, HALF])
        consts_in = m.sem("consts_in")
        loaded = [m.sem(f"loaded{i}") for i in range(2)]
        biased = m.sem("biased")
        multiplied = m.sem("multiplied")
        added = m.sem("added")
        stored = [m.sem(f"stored{i}") for i in range(2)]
        block = ctx.enter_context(nc.Block())

        @block.sync
        def _(sp):
            sp.dma_start(w[:], wo_in.rearrange("(c p) n -> p c n", p=P)).then_inc(consts_in, 16)
            sp.dma_start(bo[:], bo_in.partition_broadcast(P)).then_inc(consts_in, 16)

            def load(b, i):
                sp.dma_start(x[:, i], scratch.x1[bass.ds(b, 1)].rearrange("a (t p) d -> p (a t) d", p=P)).then_inc(loaded[i], 16)
                sp.dma_start(att[:, i], scratch.o[bass.ds(b * (KD * CHUNKS) + LATE, KD * CHUNKS)].rearrange("s p n -> p s n")).then_inc(loaded[i], 16)

            for i in range(2):
                load(i, i)
            for b in range(B):
                i = b % 2
                sp.wait_ge(added, (b + 1) * NT)
                sp.dma_start(out[b].rearrange("(t p) d -> p t d", p=P), x[:, i]).then_inc(stored[i], 16)
                if b + 2 < B:
                    sp.wait_ge(stored[i], 16 * (b // 2 + 1))
                    load(b + 2, i)
            for i in range(2):
                sp.wait_ge(stored[i], 16 * (B // 2))

        @block.vector
        def _(dve):
            dve.wait_ge(consts_in, 32)
            with dve.Fori(0, B, 2) as b0:
                for i in range(2):
                    dve.wait_ge(loaded[i], 32 * (b0 // 2 + 1))
                    for t in range(NT):
                        n = (b0 + i) * NT + t
                        nc.vector.tensor_tensor(x[:, i, t], x[:, i, t], bo[:], ALU.add).then_inc(biased, 1)
                        dve.wait_ge(multiplied, n + 1)
                        dve.wait_ge(biased, n + 1)
                        nc.vector.tensor_tensor(x[:, i, t], x[:, i, t], y_ps[:, t % 2, 0:D], ALU.add).then_inc(added, 1)

        @block.tensor
        def _(pe):
            pe.wait_ge(consts_in, 32)
            dummy = None
            for b in range(B):
                i = b % 2
                pe.wait_ge(loaded[i], 32 * (b // 2 + 1))
                for t in range(NT):
                    n = b * NT + t
                    if n >= 2:
                        pe.wait_ge(added, n - 1)
                    for g in range(KD):
                        last = nc.tensor.matmul(y_ps[:, t % 2, 0:D], att[:, i, g * CHUNKS + t // QT, (t % QT) * P:(t % QT + 1) * P],
                                                w[:, g, :], start=(g == 0), stop=(g == KD - 1))
                    last.then_inc(multiplied, 1)


def build(nc, x, adj, wq0, bq0, wk0, bk0, wv0, bv0, beta, wq1, wk1, wv1, bv1, wo1, bo1, ident, out):
    scratch = Scratch(nc)
    project(nc, 0, x, ident, wq0, wk0, wv0, bq0, bk0, bv0, scratch)
    attend(nc, 0, adj, ident, beta, scratch)
    project(nc, 1, x, ident, wq1, wk1, wv1, None, None, bv1, scratch)
    attend(nc, 1, adj, ident, beta, scratch)
    finish(nc, wo1, bo1, scratch, out)


def kernel(**inputs):
    import numpy as np
    import concourse.bacc as bacc
    from concourse.bass_utils import run_bass_kernel_spmd

    a = {k: np.asarray(v) for k, v in inputs.items()}
    arrays = {
        "x": a["x"], "adj": a["adj"],
        "wq0": a["L0_gnn_Wq"], "bq0": a["L0_gnn_bq"].reshape(KD, P).T, "wk0": a["L0_gnn_Wk"], "bk0": a["L0_gnn_bk"].reshape(KD, P).T,
        "wv0": a["L0_gnn_Wv"], "bv0": a["L0_gnn_bv"], "beta": a["L0_gnn_beta"].reshape(1),
        "wq1": a["L1_gnn_Wq"].T, "wk1": a["L1_gnn_Wk"].T, "wv1": a["L1_gnn_Wv"].T, "bv1": a["L1_gnn_bv"],
        "wo1": a["L1_gnn_Wo"].T, "bo1": a["L1_gnn_bo"],
        "ident": np.eye(P, dtype=np.float32),
    }
    arrays = {f"in_{k}": np.ascontiguousarray(v) for k, v in arrays.items()}
    nc = bacc.Bacc("TRN2", target_bir_lowering=False, num_devices=1)
    args = [nc.dram_tensor(k, v.shape, mybir.dt.from_np(v.dtype), kind="ExternalInput").ap() for k, v in arrays.items()]
    args.append(nc.dram_tensor("out_y", (B, N, D), F32, kind="ExternalOutput").ap())
    build(nc, *args)
    r = run_bass_kernel_spmd(nc, [arrays], core_ids=[0])
    return r.results[0]["out_y"]
```

```python
from contextlib import ExitStack, contextmanager

import concourse.bass as bass
from concourse import mybir

F32 = mybir.dt.float32
F32R = mybir.dt.float32r
ALU = mybir.AluOpType
ACT = mybir.ActivationFunctionType

P = 128
B, N, D, H = 8, 1024, 384, 12
HD = D // H
NT = N // P
KD = D // P
HG = P // HD
HALF = 512
GROUPS = B * KD
CHUNK = 256
CHUNKS = N // CHUNK
QT = CHUNK // P
TILES = CHUNKS * HG * QT
CT = HG * QT
BIAS_STEPS = ((), (0,), (1,), (2,), (3, 4), (5,), (), ())
INVERT_AT = 2
DIVIDE_AT = 5
TRAIL = 4
LATE = 2
SLOTS = GROUPS * CHUNKS + LATE
EPS = 1e-5
MASKED = -9.0e15
BIG = 3.0e38
GONE = -1.0e30
TINY = 1.0e-30


class Scratch:

    def __init__(self, nc):
        self.q = nc.dram_tensor("q_parts", [GROUPS, 2, P, N], F32).ap()
        self.k = nc.dram_tensor("k_parts", [GROUPS, 2, P, N], F32).ap()
        self.v = nc.dram_tensor("v_rows", [GROUPS, P, NT * P], F32).ap()
        self.o = nc.dram_tensor("attended_t", [SLOTS, P, CHUNK], F32).ap()
        self.flags = nc.dram_tensor("maybe_zero_rows", [P, TILES], F32).ap()
        self.x1 = nc.dram_tensor("x_between", [B, N, D], F32).ap()


class Mem:

    def __init__(self, nc, ctx, tag):
        self.nc, self.ctx, self.tag = nc, ctx, tag
        self.holds = self.sem("holds")

    def hold(self, eng, sem, value):
        eng.wait_ge(sem, value)
        eng.sem_inc(self.holds, 1)

    def sb(self, name, shape, dt=F32):
        return self.ctx.enter_context(self.nc.sbuf_tensor(f"{name}_{self.tag}", shape, dt))

    def ps(self, name, shape):
        return self.ctx.enter_context(self.nc.psum_tensor(f"{name}_{self.tag}", shape, F32))

    def sem(self, name):
        return self.ctx.enter_context(self.nc.semaphore(f"{name}_{self.tag}"))


def project(nc, layer, x_in, ident_in, wq_in, wk_in, wv_in, bq_in, bk_in, bv_in, scratch):
    q_scale = float(HD) ** -0.5 if layer == 0 else float(D) ** -0.5
    UNITS = 2 * KD * 2
    with ExitStack() as ctx:
        m = Mem(nc, ctx, f"project{layer}")
        ident = m.sb("ident", [P, P])
        w = m.sb("w", [P, 3, KD, D])
        qk_bias = m.sb("qk_bias", [P, 2, KD])
        v_bias = m.sb("v_bias", [P, D])
        x = m.sb("x", [P, NT, D])
        att = m.sb("att", [P, KD * CHUNKS, CHUNK])
        h = m.sb("h", [P, NT, D])
        stats = m.sb("stats", [P, NT, 6])
        moments = m.sb("moments", [P, NT, 2])
        var = m.sb("var", [P, NT])
        std = m.sb("std", [P, NT])
        rstd = m.sb("rstd", [P, NT])
        h_t = m.sb("h_t", [P, KD, N])
        full = m.sb("full", [P, 2, HALF])
        high = m.sb("high", [P, 2, HALF], F32R)
        low = m.sb("low", [P, 2, HALF], F32R)
        v_out = m.sb("v_out", [P, 2, D])
        turn_ps = m.ps("turn_ps", [P, 2, HALF])
        att_ps = m.ps("att_ps", [P, 2, HALF])
        qk_ps = m.ps("qk_ps", [P, 2, HALF])
        v_ps = m.ps("v_ps", [P, 2, HALF])

        consts_in = m.sem("consts_in")
        x_loaded = m.sem("x_loaded")
        x_free = m.sem("x_free")
        if layer == 1:
            att_loaded = m.sem("att_loaded")
            att_turned = m.sem("att_turned")
            x_added = m.sem("x_added")
            x1_stored = m.sem("x1_stored")
        stats_done = m.sem("stats_done")
        moments_done = m.sem("moments_done")
        var_ready = m.sem("var_ready")
        std_ready = m.sem("std_ready")
        rstd_ready = m.sem("rstd_ready")
        h_ready = m.sem("h_ready")
        h_turned = m.sem("h_turned")
        h_t_ready = m.sem("h_t_ready")
        qk_done = m.sem("qk_done")
        full_ready = m.sem("full_ready")
        high_ready = m.sem("high_ready")
        low_ready = m.sem("low_ready")
        qk_stored = [m.sem(f"qk_stored{i}") for i in range(2)]
        v_done = m.sem("v_done")
        v_ready = m.sem("v_ready")
        v_stored = [m.sem(f"v_stored{i}") for i in range(2)]
        N_CONSTS = 4 + (3 if layer == 0 else 1)

        block = ctx.enter_context(nc.Block())

        @block.sync
        def _(sp):
            for t, src in enumerate((wq_in, wk_in, wv_in)):
                sp.dma_start(w[:, t], src.rearrange("(c p) n -> p c n", p=P)).then_inc(consts_in, 16)
            sp.dma_start(ident[:], ident_in).then_inc(consts_in, 16)
            sp.dma_start(v_bias[:], bv_in.partition_broadcast(P)).then_inc(consts_in, 16)
            if layer == 0:
                sp.dma_start(qk_bias[:, 0, :], bq_in).then_inc(consts_in, 16)
                sp.dma_start(qk_bias[:, 1, :], bk_in).then_inc(consts_in, 16)
            with sp.Fori(0, B) as b:
                if layer == 1:
                    m.hold(sp, x_added, (b + 1) * NT)
                    sp.dma_start(scratch.x1[bass.ds(b, 1)].rearrange("a (t p) d -> p (a t) d", p=P), x[:]).then_inc(x1_stored, 16)
                for u in range(UNITS):
                    tensor, fg, half = u // (2 * KD), u // 2 % KD, u % 2
                    dst = (scratch.q, scratch.k)[tensor]
                    for part, tile, ready in ((0, high, high_ready), (1, low, low_ready)):
                        m.hold(sp, ready, b * UNITS + u + 1)
                        sp.dma_start(dst[bass.ds(b * KD + fg, 1), part, :, half * HALF:(half + 1) * HALF].rearrange("a p n -> (a p) n"),
                                     tile[:, u % 2].bitcast(F32)).then_inc(qk_stored[u % 2], 16)
                for t in range(NT):
                    m.hold(sp, v_ready, b * NT + t + 1)
                    sp.dma_start(scratch.v[bass.ds(b * KD, KD), :, t * P:(t + 1) * P].rearrange("g p f -> p g f"),
                                 v_out[:, t % 2].rearrange("p (g f) -> p g f", g=KD)).then_inc(v_stored[t % 2], 16)
            for i in range(2):
                sp.wait_ge(qk_stored[i], 32 * (UNITS // 2 * B + 1))
                sp.wait_ge(v_stored[i], 16 * (NT // 2 * B + 1))
            if layer == 1:
                sp.wait_ge(x1_stored, 16 * (B + 1))

        @block.gpsimd
        def _(pool):
            pool.nop().then_inc(x_free, NT)
            for i in range(2):
                pool.nop().then_inc(qk_stored[i], 32)
                pool.nop().then_inc(v_stored[i], 16)
            if layer == 1:
                pool.nop().then_inc(x1_stored, 16)
            with pool.Fori(0, B) as b:
                pool.wait_ge(x_free, NT * (b + 1))
                if layer == 1:
                    pool.wait_ge(x1_stored, 16 * (b + 1))
                pool.dma_start(x[:], x_in[bass.ds(b, 1)].rearrange("a (t p) d -> p (a t) d", p=P)).then_inc(x_loaded, 16)
                if layer == 1:
                    pool.dma_start(att[:], scratch.o[bass.ds(b * (KD * CHUNKS) + LATE, KD * CHUNKS)].rearrange("s p n -> p s n")).then_inc(att_loaded, 16)

        @block.scalar
        def _(act):
            with act.Fori(0, B) as b:
                act.wait_ge(var_ready, b + 1)
                nc.scalar.activation(std[:], var[:], ACT.Sqrt).then_inc(std_ready, 1)
                for t in range(NT):
                    act.wait_ge(h_turned, b * NT + t + 1)
                    nc.scalar.activation(h_t[:, :, t * P:(t + 1) * P], turn_ps[:, t % 2, 0:D].rearrange("p (c n) -> p c n", c=KD),
                                         ACT.Relu).then_inc(h_t_ready, 1)
                for u in range(UNITS):
                    act.wait_ge(full_ready, b * UNITS + u + 1)
                    act.wait_ge(qk_stored[u % 2], 32 * (b * (UNITS // 2) + u // 2 + 1))
                    nc.scalar.activation(high[:, u % 2], full[:, u % 2], ACT.Copy).then_inc(high_ready, 1)

        @block.vector
        def _(dve):
            dve.wait_ge(consts_in, 16 * N_CONSTS)
            with dve.Fori(0, B) as b:
                dve.wait_ge(x_loaded, 16 * (b + 1))
                if layer == 1:
                    for t in range(NT):
                        dve.wait_ge(att_turned, b * NT + t + 1)
                        nc.vector.tensor_tensor(x[:, t], x[:, t], att_ps[:, t % 2, 0:D], ALU.add).then_inc(x_added, 1)
                for t in range(NT):
                    if layer == 1:
                        dve.wait_ge(x_added, b * NT + t + 1)
                    nc.vector.bn_stats(stats[:, t], x[:, t]).then_inc(stats_done, 1)
                for t in range(NT):
                    m.hold(dve, stats_done, b * NT + t + 1)
                    nc.vector.bn_aggr(moments[:, t], stats[:, t]).then_inc(moments_done, 1)
                dve.wait_ge(moments_done, (b + 1) * NT)
                nc.vector.tensor_scalar(var[:], moments[:, :, 1], EPS, None, ALU.add).then_inc(var_ready, 1)
                dve.wait_ge(std_ready, b + 1)
                nc.vector.reciprocal(rstd[:], std[:]).then_inc(rstd_ready, 1)
                dve.wait_ge(rstd_ready, b + 1)
                for t in range(NT):
                    nc.vector.tensor_scalar(h[:, t], x[:, t], moments[:, t, 0:1], rstd[:, t:t + 1], ALU.subtract, ALU.mult).then_inc(h_ready, 1)
                dve.wait_ge(h_ready, (b + 1) * NT)
                dve.nop().then_inc(x_free, NT)
                for u in range(UNITS):
                    tensor, fg = u // (2 * KD), u // 2 % KD
                    dve.wait_ge(qk_done, b * UNITS + u + 1)
                    dve.wait_ge(qk_stored[u % 2], 32 * (b * (UNITS // 2) + u // 2 + 1))
                    bias = qk_bias[:, tensor, fg:fg + 1] if layer == 0 else 0.0
                    nc.vector.tensor_scalar(full[:, u % 2], qk_ps[:, u % 2], bias, 1.0 if tensor else q_scale,
                                            ALU.add, ALU.mult).then_inc(full_ready, 1)
                    dve.wait_ge(high_ready, b * UNITS + u + 1)
                    nc.vector.tensor_tensor(low[:, u % 2], full[:, u % 2], high[:, u % 2].bitcast(F32), ALU.subtract).then_inc(low_ready, 1)
                for t in range(NT):
                    dve.wait_ge(v_done, b * NT + t + 1)
                    dve.wait_ge(v_stored[t % 2], 16 * (b * (NT // 2) + t // 2 + 1))
                    nc.vector.tensor_tensor(v_out[:, t % 2], v_ps[:, t % 2, 0:D], v_bias[:], ALU.add).then_inc(v_ready, 1)

        @block.tensor
        def _(pe):
            pe.wait_ge(consts_in, 16 * N_CONSTS)
            with pe.Fori(0, B) as b:
                if layer == 1:
                    pe.wait_ge(att_loaded, 16 * (b + 1))
                    for t in range(NT):
                        if t >= 2:
                            pe.wait_ge(x_added, b * NT + t - 1)
                        for g in range(KD):
                            last = nc.tensor.transpose(att_ps[:, t % 2, g * P:(g + 1) * P],
                                                       att[:, g * CHUNKS + t // QT, (t % QT) * P:(t % QT + 1) * P], ident[:])
                        last.then_inc(att_turned, 1)
                for t in range(NT):
                    pe.wait_ge(h_ready, b * NT + t + 1)
                    if t >= 2:
                        pe.wait_ge(h_t_ready, b * NT + t - 1)
                    for c in range(KD):
                        last = nc.tensor.transpose(turn_ps[:, t % 2, c * P:(c + 1) * P], h[:, t, c * P:(c + 1) * P], ident[:])
                    last.then_inc(h_turned, 1)
                pe.wait_ge(h_t_ready, (b + 1) * NT)
                for u in range(UNITS):
                    tensor, fg, half = u // (2 * KD), u // 2 % KD, u % 2
                    if u >= 2:
                        pe.wait_ge(full_ready, b * UNITS + u - 1)
                    for c in range(KD):
                        last = nc.tensor.matmul(qk_ps[:, u % 2], w[:, tensor, c, fg * P:(fg + 1) * P],
                                                h_t[:, c, half * HALF:(half + 1) * HALF], start=(c == 0), stop=(c == KD - 1))
                    last.then_inc(qk_done, 1)
                for t in range(NT):
                    if t >= 2:
                        pe.wait_ge(v_ready, b * NT + t - 1)
                    for c in range(KD):
                        last = nc.tensor.matmul(v_ps[:, t % 2, 0:D], h_t[:, c, t * P:(t + 1) * P], w[:, 2, c, :],
                                                start=(c == 0), stop=(c == KD - 1))
                    last.then_inc(v_done, 1)


def attend(nc, layer, adj_in, ident_in, beta_in, scratch, guarded=False):
    with ExitStack() as ctx:
        m = Mem(nc, ctx, f"attend{layer}" + "_guarded" * guarded)
        ident = m.sb("ident", [P, P])
        ones = m.sb("ones", [P, HD])
        beta = m.sb("beta", [P, 1])
        q_st = m.sb("q_st", [P, HG, N], F32R)
        k_st = m.sb("k_st", [P, HG, N], F32R)
        v_now = m.sb("v_now", [P, NT, P])
        v_kept = m.sb("v_kept", [P, NT, P])
        bias = m.sb("bias", [P, NT, N])
        rows = m.sb("rows", [P, 4, N])
        neg_max = m.sb("neg_max", [P, TILES])
        if layer == 0:
            adj = m.sb("adj", [P, QT, N])
            masked = m.sb("masked", [P, QT, N])
        if layer == 1 and not guarded:
            maybe_zero = m.sb("maybe_zero", [P, TILES])
        if guarded:
            any_flag = m.sb("any_flag", [1, 1])
            decision = m.sb("decision", [1, 1], mybir.dt.int32)
            spare = m.sb("spare", [P, N])
            neg_min = m.sb("neg_min", [P, TILES])
            max_zero = m.sb("max_zero", [P, TILES])
            all_zero = m.sb("all_zero", [P, TILES])
        shift = m.sb("shift", [P, TILES]) if guarded else neg_max
        probs = m.sb("probs", [P, 2, HG, NT, CHUNK])
        pairs = m.sb("pairs", [P, 2, HG, NT // 2, CHUNK])
        undivided = m.sb("undivided", [P, 2, HALF])
        out_t = m.sb("out_t", [P, 2, CHUNK])
        s_ps = m.ps("s_ps", [P, 2, N])
        t_ps = m.ps("t_ps", [P, 2, HALF])
        o_ps = m.ps("o_ps", [P, 2, HALF])

        consts_in = m.sem("consts_in")
        inited = m.sem("inited")
        qk_loaded = [m.sem(f"qk_loaded{j}") for j in range(HG)]
        adj_loaded = [m.sem(f"adj_loaded{c}") for c in range(CHUNKS)]
        v_loaded = m.sem("v_loaded")
        v_copied = m.sem("v_copied")
        scored = m.sem("scored")
        negated = m.sem("negated")
        shift_ready = score_read = negated
        if guarded:
            checked = score_read = m.sem("checked")
            max_zero_ready = m.sem("max_zero_ready")
            all_zero_ready = m.sem("all_zero_ready")
            shift_ready = m.sem("shift_ready")
            flags_loaded = m.sem("flags_loaded")
            reduced = m.sem("reduced")
            decided = m.sem("decided")
        elif layer == 1:
            flagged = m.sem("flagged")
            flags_stored = m.sem("flags_stored")
        else:
            positive_ready = m.sem("positive_ready")
            sign_ready = m.sem("sign_ready")
            masked_ready = m.sem("masked_ready")
            bias_ready = m.sem("bias_ready")
        shifted_ready = m.sem("shifted_ready")
        turned = m.sem("turned")
        exp_done = m.sem("exp_done")
        paired = m.sem("paired")
        pv_done = m.sem("pv_done")
        inv_ready = m.sem("inv_ready")
        taken = m.sem("taken")
        out_ready = m.sem("out_ready")
        out_stored = [m.sem(f"out_stored{i}") for i in range(2)]
        QK_IN = 16 * 8
        flags = rows[0:1].rearrange("a b n -> a (b n)")[:, 0:P * TILES]

        @contextmanager
        def if_needed(eng):
            if guarded:
                m.hold(eng, decided, 1)
                needed = eng.value_load(decision[0:1, 0:1], min_val=0, max_val=1)
                with eng.If(needed > 0):
                    yield
            else:
                yield

        block = ctx.enter_context(nc.Block())

        @block.sync
        def _(sp):
            def load_qk(r, j):
                heads = slice(j * HD, (j + 1) * HD)
                for row, part in enumerate((0, 0, 1, 1)):
                    sp.dma_start(q_st[row * HD:(row + 1) * HD, j].bitcast(F32),
                                 scratch.q[bass.ds(r, 1), part, heads, :].rearrange("a p n -> (a p) n")).then_inc(qk_loaded[j], 16)
                for row, part in enumerate((0, 1, 0, 1)):
                    sp.dma_start(k_st[row * HD:(row + 1) * HD, j].bitcast(F32),
                                 scratch.k[bass.ds(r, 1), part, heads, :].rearrange("a p n -> (a p) n")).then_inc(qk_loaded[j], 16)

            def load_adj(b, c):
                dst = adj[:] if layer == 0 else bias[:, c * QT:(c + 1) * QT]
                sp.dma_start(dst, adj_in[bass.ds(b, 1), c * CHUNK:(c + 1) * CHUNK, :].rearrange("a (t p) n -> p (a t) n", p=P)).then_inc(adj_loaded[c], 16)

            def load_v(r):
                sp.dma_start(v_now[:], scratch.v[bass.ds(r, 1)].rearrange("a p (t f) -> (a p) t f", t=NT)).then_inc(v_loaded, 16)

            def store(n, i):
                m.hold(sp, out_ready, n + LATE + 1)
                sp.dma_start(scratch.o[bass.ds(n, 1)].rearrange("a p n -> (a p) n"), out_t[:, i]).then_inc(out_stored[i], 16)

            def group(r, next_r, refill):
                if refill is not None and layer == 0:
                    m.hold(sp, bias_ready, (refill[0] + 1) * CHUNKS * QT)
                    load_adj(refill[1], 0)
                for c in range(CHUNKS):
                    if c == CHUNKS - 1:
                        for j in range(HG // 2):
                            m.hold(sp, scored, r * TILES + c * CT + (j + 1) * QT)
                            load_qk(next_r, j)
                    store(r * CHUNKS + c, c % 2)
                    if c == CHUNKS - 1:
                        for j in range(HG // 2, HG):
                            m.hold(sp, scored, r * TILES + c * CT + (j + 1) * QT)
                            load_qk(next_r, j)
                    if refill is not None:
                        this_b, next_b = refill
                        if layer == 1:
                            m.hold(sp, score_read, r * TILES + (c + 1) * CT + guarded)
                            load_adj(next_b, c)
                        elif c < CHUNKS - 1:
                            m.hold(sp, bias_ready, ((this_b + 1) * CHUNKS + c + 1) * QT)
                            load_adj(next_b, c + 1)
                m.hold(sp, pv_done, r * CHUNKS + CHUNKS - 2 + LATE + 1)
                m.hold(sp, v_copied, r + 2)
                load_v(next_r)

            if guarded:
                sp.dma_start(flags, scratch.flags.rearrange("(a p) t -> a (p t)", a=1)).then_inc(flags_loaded, 16)
            with if_needed(sp):
                sp.dma_start(ident[:], ident_in).then_inc(consts_in, 16)
                sp.dma_start(beta[:], beta_in.partition_broadcast(P)).then_inc(consts_in, 16)
                for c in range(CHUNKS):
                    if c == 1:
                        for j in range(HG):
                            load_qk(0, j)
                        load_v(0)
                    if layer == 0 and c:
                        sp.wait_ge(bias_ready, c * QT)
                    load_adj(0, c)
                with sp.Fori(0, B - 1) as b:
                    with sp.Fori(0, KD - 1) as g:
                        group(b * KD + g, b * KD + g + 1, None)
                    group(b * KD + KD - 1, b * KD + KD, (b, b + 1))
                for r in range(GROUPS - KD, GROUPS):
                    group(r, min(r + 1, GROUPS - 1), (B - 1, B - 1) if r == GROUPS - 1 else None)
                for i in range(LATE):
                    store(GROUPS * CHUNKS + i, i)
                for i in range(2):
                    sp.wait_ge(out_stored[i], 16 * (SLOTS // 2 + 1))
                for j in range(HG):
                    sp.wait_ge(qk_loaded[j], QK_IN * (GROUPS + 1))
                for c in range(CHUNKS):
                    sp.wait_ge(adj_loaded[c], 16 * (B + 1))
                sp.wait_ge(v_loaded, 16 * (GROUPS + 1))
                if layer == 1 and not guarded:
                    sp.wait_ge(flagged, GROUPS + 1)
                    sp.dma_start(scratch.flags, maybe_zero[:]).then_inc(flags_stored, 16)
                    sp.wait_ge(flags_stored, 16)

        @block.gpsimd
        def _(pool):
            def divide(n, n_half, i):
                pool.wait_ge(inv_ready, n * 2 + 2)
                pool.wait_ge(out_stored[i], 16 * (n_half + 1))
                nc.gpsimd.tensor_tensor(out_t[:, i], undivided[:, i, 0:CHUNK], undivided[:, i, CHUNK:], ALU.mult).then_inc(out_ready, 1)

            with if_needed(pool):
                nc.gpsimd.memset(probs[:, 0, :, 0], 1.0).then_inc(inited, 1)
                nc.gpsimd.memset(v_kept[:], 0.0).then_inc(inited, 1)
                nc.gpsimd.memset(ones[:], 1.0).then_inc(inited, 1)
                nc.gpsimd.memset(probs[:, 1], 1.0).then_inc(inited, 1)
                nc.gpsimd.memset(pairs[:], 2.0).then_inc(inited, 1)
                with pool.Fori(0, GROUPS) as r:
                    for t in range(TILES):
                        m.hold(pool, shift_ready, r * TILES + t + 1)
                        nc.gpsimd.tensor_scalar(rows[:, t % 4], rows[:, t % 4], -1.0, shift[:, t:t + 1],
                                                ALU.mult, ALU.add).then_inc(shifted_ready, 1)
                        if t % CT == DIVIDE_AT:
                            c = t // CT
                            divide(r * CHUNKS + c, r * (CHUNKS // 2) + c // 2, c % 2)
                for i in range(LATE):
                    n = GROUPS * CHUNKS + i
                    divide(n, n // 2, i)

        @block.scalar
        def _(act):
            def bias_part(b, c, step):
                u, op = step // 3, step % 3
                n = (b * CHUNKS + c) * QT + u
                if op == 0:
                    act.wait_ge(adj_loaded[c], 16 * (b + 1))
                    nc.scalar.activation(adj[:, u], adj[:, u], ACT.Relu).then_inc(positive_ready, 1)
                elif op == 1:
                    act.wait_ge(positive_ready, n + 1)
                    nc.scalar.activation(masked[:, u], adj[:, u], ACT.Sign).then_inc(sign_ready, 1)
                else:
                    act.wait_ge(sign_ready, n + 1)
                    nc.scalar.activation(masked[:, u], masked[:, u], ACT.Copy, bias=MASKED, scale=-MASKED).then_inc(masked_ready, 1)

            def take(n, i):
                act.wait_ge(pv_done, n + 1)
                act.wait_ge(out_ready, n + LATE - 1)
                nc.scalar.activation(undivided[:, i], o_ps[:, i], ACT.Copy).then_inc(taken, 1)

            def group(r, refill_b):
                for t in range(TILES):
                    c, j, u = t // CT, t // QT % HG, t % QT
                    if t % CT == 0:
                        act.wait_ge(pv_done, r * CHUNKS + c - 2 + LATE + 1)
                    for half in range(2):
                        keys = slice(half * NT // 2, (half + 1) * NT // 2)
                        act.wait_ge(turned, (r * TILES + t) * 2 + half + 1)
                        nc.scalar.activation(probs[:, c % 2, j, keys, u * P:(u + 1) * P],
                                             t_ps[:, half].rearrange("p (k n) -> p k n", k=NT // 2), ACT.Exp).then_inc(exp_done, 1)
                    if t % CT == 0:
                        take(r * CHUNKS + c, c % 2)
                    elif refill_b is not None and layer == 0:
                        for step in BIAS_STEPS[t % CT]:
                            bias_part(refill_b, c, step)

            with if_needed(act):
                act.nop().then_inc(exp_done, 2 * TRAIL)
                act.nop().then_inc(taken, 1)
                for i in range(2):
                    act.nop().then_inc(out_stored[i], 16)
                act.wait_ge(consts_in, 32)
                if layer == 0:
                    for c in range(CHUNKS):
                        if c:
                            act.wait_ge(bias_ready, c * QT)
                        for step in range(3 * QT):
                            bias_part(0, c, step)
                with act.Fori(0, B) as b:
                    with act.Fori(0, KD - 1) as g:
                        group(b * KD + g, None)
                    group(b * KD + KD - 1, b + 1)
                for i in range(LATE):
                    take(GROUPS * CHUNKS + i, i)

        @block.vector
        def _(dve):
            def make_bias(b, c, u):
                m.hold(dve, masked_ready, (b * CHUNKS + c) * QT + u + 1)
                nc.vector.scalar_tensor_tensor(bias[:, c * QT + u], adj[:, u], beta[:, 0:1], masked[:, u],
                                               ALU.mult, ALU.add).then_inc(bias_ready, 1)

            def invert(n, i, half):
                dve.wait_ge(taken, n + 2)
                part = undivided[:, i, CHUNK + half * P:CHUNK + (half + 1) * P]
                nc.vector.reciprocal(part, part).then_inc(inv_ready, 1)

            def group(b, r, refill_b):
                for t in range(TILES):
                    c, qi = t // CT, t // CT * QT + t % QT
                    n = r * TILES + t
                    if layer == 1 and t % CT == 0:
                        dve.wait_ge(adj_loaded[c], 16 * (b + 1))
                    if t == 0 and layer == 1 and not guarded:
                        dve.wait_ge(flagged, r + 1)
                    m.hold(dve, scored, n + 1)
                    nc.vector.tensor_tensor_reduce(out=rows[:, t % 4], in0=s_ps[:, t % 2], in1=bias[:, qi], scale=-1.0, scalar=BIG,
                                                   op0=ALU.add, op1=ALU.min, accum_out=neg_max[:, t:t + 1]).then_inc(negated, 1)
                    if guarded:
                        dve.wait_ge(negated, n + 1)
                        m.hold(dve, checked, n + 1)
                        nc.vector.tensor_tensor_reduce(out=spare[:], in0=s_ps[:, t % 2], in1=bias[:, qi], scale=-1.0, scalar=-BIG,
                                                       op0=ALU.add, op1=ALU.max, accum_out=neg_min[:, t:t + 1]).then_inc(checked, 1)
                        nc.vector.tensor_scalar(max_zero[:, t:t + 1], neg_max[:, t:t + 1], 0.0, GONE, ALU.is_equal, ALU.mult).then_inc(max_zero_ready, 1)
                        dve.wait_ge(checked, n + 2)
                        dve.wait_ge(max_zero_ready, n + 1)
                        nc.vector.scalar_tensor_tensor(all_zero[:, t:t + 1], neg_min[:, t:t + 1], 0.0, max_zero[:, t:t + 1],
                                                       ALU.is_equal, ALU.mult).then_inc(all_zero_ready, 1)
                        dve.wait_ge(all_zero_ready, n + 1)
                        nc.vector.tensor_tensor(shift[:, t:t + 1], all_zero[:, t:t + 1], neg_max[:, t:t + 1], ALU.add).then_inc(shift_ready, 1)
                    if t % QT == 1:
                        before = (t - TRAIL) % TILES
                        buf, j = before // CT % 2, before // QT % HG
                        dve.wait_ge(exp_done, 2 * (n + 1))
                        nc.vector.tensor_tensor(pairs[:, buf, j], probs[:, buf, j, 0:NT // 2], probs[:, buf, j, NT // 2:], ALU.add).then_inc(paired, 1)
                    if t % CT in (INVERT_AT, 2 * INVERT_AT):
                        invert(r * CHUNKS + c, c % 2, t % CT // INVERT_AT - 1)
                    if t == 2 * CT:
                        dve.wait_ge(v_loaded, 16 * (r + 1))
                        dve.wait_ge(pv_done, r * CHUNKS - 1 + LATE + 1)
                        nc.vector.tensor_copy(v_kept[:], v_now[:]).then_inc(v_copied, 1)
                    if refill_b is not None and layer == 0 and t // QT % HG == HG - 1:
                        dve.wait_ge(negated, n + 1)
                        make_bias(refill_b, c, t % QT)
                if layer == 1 and not guarded:
                    dve.wait_ge(negated, r * TILES + TILES)
                    nc.vector.scalar_tensor_tensor(maybe_zero[:], neg_max[:], 0.0, maybe_zero[:], ALU.is_equal, ALU.max).then_inc(flagged, 1)

            if guarded:
                dve.wait_ge(flags_loaded, 16)
                nc.vector.reduce_max(any_flag[:], flags, axis=mybir.AxisListType.X).then_inc(reduced, 1)
                dve.wait_ge(reduced, 1)
                nc.vector.tensor_copy(decision[:], any_flag[:]).then_inc(decided, 1)
            with if_needed(dve):
                dve.nop().then_inc(out_ready, LATE)
                dve.nop().then_inc(v_copied, 1)
                if guarded:
                    dve.nop().then_inc(checked, 1)
                if layer == 1 and not guarded:
                    nc.vector.memset(maybe_zero[:], 0.0).then_inc(flagged, 1)
                dve.wait_ge(consts_in, 32)
                dve.wait_ge(inited, 5)
                if layer == 0:
                    for c in range(CHUNKS):
                        for u in range(QT):
                            make_bias(0, c, u)
                    dve.wait_ge(bias_ready, CHUNKS * QT)
                with dve.Fori(0, B) as b:
                    with dve.Fori(0, KD - 1) as g:
                        group(b, b * KD + g, None)
                    group(b, b * KD + KD - 1, b + 1)
                for j in range(HG - TRAIL // QT, HG):
                    dve.wait_ge(exp_done, 2 * (GROUPS * TILES + TRAIL))
                    nc.vector.tensor_tensor(pairs[:, 1, j], probs[:, 1, j, 0:NT // 2], probs[:, 1, j, NT // 2:], ALU.add).then_inc(paired, 1)
                for i in range(LATE):
                    for half in range(2):
                        invert(GROUPS * CHUNKS + i, i, half)

        @block.tensor
        def _(pe):
            def score(t, n):
                c, j, u = t // CT, t // QT % HG, t % QT
                queries = slice((c * QT + u) * P, (c * QT + u + 1) * P)
                for half in range(2):
                    last = nc.tensor.matmul(s_ps[:, t % 2, half * HALF:(half + 1) * HALF], q_st[:, j, queries],
                                            k_st[:, j, half * HALF:(half + 1) * HALF], start=True, stop=True)
                last.then_inc(scored, 1)

            def values(i, v, kt):
                for j in range(HG):
                    last = nc.tensor.matmul(o_ps[j * HD:(j + 1) * HD, i, 0:CHUNK], v[:, kt, j * HD:(j + 1) * HD],
                                            probs[:, i, j, kt], start=(kt == 0), stop=(kt == NT - 1), skip_group_check=True)
                return last

            def sums(i, kp):
                for j in range(HG):
                    last = nc.tensor.matmul(o_ps[j * HD:(j + 1) * HD, i, CHUNK:], ones[:], pairs[:, i, j, kp],
                                            start=False, stop=(kp == NT // 2 - 1), skip_group_check=True)
                return last

            with if_needed(pe):
                pe.wait_ge(inited, 5)
                pe.wait_ge(consts_in, 32)
                values(0, v_kept, 0)
                sums(0, 0).then_inc(pv_done, 1)
                for t in range(2):
                    pe.wait_ge(qk_loaded[t // QT], QK_IN)
                    score(t, t)
                with pe.Fori(0, GROUPS) as r:
                    for t in range(TILES):
                        c = t // CT
                        n = r * TILES + t
                        ahead = t + 2
                        if ahead % TILES < CT and ahead % QT == 0:
                            pe.wait_ge(qk_loaded[ahead % TILES // QT], QK_IN * (r + 1 + ahead // TILES))
                        pe.wait_ge(score_read, n + 1 + guarded)
                        score(ahead % TILES, n + 2)
                        pe.wait_ge(shifted_ready, n + 1)
                        for half in range(2):
                            pe.wait_ge(exp_done, (n + TRAIL - 1) * 2 + half + 1)
                            for k in range(NT // 2):
                                kt = half * NT // 2 + k
                                last = nc.tensor.transpose(t_ps[:, half, k * P:(k + 1) * P], rows[:, t % 4, kt * P:(kt + 1) * P], ident[:])
                            last.then_inc(turned, 1)
                        if t % CT == 0:
                            pe.wait_ge(exp_done, 2 * (n + TRAIL))
                            pe.wait_ge(taken, r * CHUNKS + c + 1)
                            if c == 0:
                                pe.wait_ge(v_copied, r + 1)
                            if c == 1:
                                pe.wait_ge(v_loaded, 16 * (r + 1))
                        kt = t % CT
                        values((c + 1) % 2, v_now if c else v_kept, kt)
                        if kt >= NT // 2:
                            if kt == NT // 2:
                                pe.wait_ge(paired, (r * CHUNKS + c) * HG + HG // 2)
                            last = sums((c + 1) % 2, kt - NT // 2)
                        if kt == NT - 1:
                            last.then_inc(pv_done, 1)
                pe.wait_ge(exp_done, 2 * (GROUPS * TILES + TRAIL))
                pe.wait_ge(taken, GROUPS * CHUNKS + 1)
                pe.wait_ge(v_copied, GROUPS + 1)
                for kt in range(NT):
                    values(1, v_kept, kt)
                pe.wait_ge(paired, GROUPS * CHUNKS * HG + HG // 2)
                for kp in range(NT // 2):
                    last = sums(1, kp)
                last.then_inc(pv_done, 1)


def finish(nc, wo_in, bo_in, scratch, out):
    with ExitStack() as ctx:
        m = Mem(nc, ctx, "finish")
        w = m.sb("w", [P, KD, D])
        bo = m.sb("bo", [P, D])
        x = m.sb("x", [P, 2, NT, D])
        att = m.sb("att", [P, 2, KD * CHUNKS, CHUNK])
        y_ps = m.ps("y_ps", [P, 2, HALF])
        consts_in = m.sem("consts_in")
        loaded = [m.sem(f"loaded{i}") for i in range(2)]
        biased = m.sem("biased")
        multiplied = m.sem("multiplied")
        added = m.sem("added")
        stored = [m.sem(f"stored{i}") for i in range(2)]
        block = ctx.enter_context(nc.Block())

        @block.sync
        def _(sp):
            sp.dma_start(w[:], wo_in.rearrange("(c p) n -> p c n", p=P)).then_inc(consts_in, 16)
            sp.dma_start(bo[:], bo_in.partition_broadcast(P)).then_inc(consts_in, 16)

            def load(b, i):
                sp.dma_start(x[:, i], scratch.x1[bass.ds(b, 1)].rearrange("a (t p) d -> p (a t) d", p=P)).then_inc(loaded[i], 16)
                sp.dma_start(att[:, i], scratch.o[bass.ds(b * (KD * CHUNKS) + LATE, KD * CHUNKS)].rearrange("s p n -> p s n")).then_inc(loaded[i], 16)

            for i in range(2):
                load(i, i)
            for b in range(B):
                i = b % 2
                sp.wait_ge(added, (b + 1) * NT)
                sp.dma_start(out[b].rearrange("(t p) d -> p t d", p=P), x[:, i]).then_inc(stored[i], 16)
                if b + 2 < B:
                    sp.wait_ge(stored[i], 16 * (b // 2 + 1))
                    load(b + 2, i)
            for i in range(2):
                sp.wait_ge(stored[i], 16 * (B // 2))

        @block.vector
        def _(dve):
            dve.wait_ge(consts_in, 32)
            with dve.Fori(0, B, 2) as b0:
                for i in range(2):
                    dve.wait_ge(loaded[i], 32 * (b0 // 2 + 1))
                    for t in range(NT):
                        n = (b0 + i) * NT + t
                        nc.vector.tensor_tensor(x[:, i, t], x[:, i, t], bo[:], ALU.add).then_inc(biased, 1)
                        dve.wait_ge(multiplied, n + 1)
                        dve.wait_ge(biased, n + 1)
                        nc.vector.tensor_tensor(x[:, i, t], x[:, i, t], y_ps[:, t % 2, 0:D], ALU.add).then_inc(added, 1)

        @block.tensor
        def _(pe):
            pe.wait_ge(consts_in, 32)
            dummy = None
            for b in range(B):
                i = b % 2
                pe.wait_ge(loaded[i], 32 * (b // 2 + 1))
                for t in range(NT):
                    n = b * NT + t
                    if n >= 2:
                        pe.wait_ge(added, n - 1)
                    for g in range(KD):
                        last = nc.tensor.matmul(y_ps[:, t % 2, 0:D], att[:, i, g * CHUNKS + t // QT, (t % QT) * P:(t % QT + 1) * P],
                                                w[:, g, :], start=(g == 0), stop=(g == KD - 1))
                    last.then_inc(multiplied, 1)


def build(nc, x, adj, wq0, bq0, wk0, bk0, wv0, bv0, beta, wq1, wk1, wv1, bv1, wo1, bo1, ident, out):
    scratch = Scratch(nc)
    project(nc, 0, x, ident, wq0, wk0, wv0, bq0, bk0, bv0, scratch)
    attend(nc, 0, adj, ident, beta, scratch)
    project(nc, 1, x, ident, wq1, wk1, wv1, None, None, bv1, scratch)
    attend(nc, 1, adj, ident, beta, scratch)
    attend(nc, 1, adj, ident, beta, scratch, guarded=True)
    finish(nc, wo1, bo1, scratch, out)


def kernel(**inputs):
    import numpy as np
    import concourse.bacc as bacc
    from concourse.bass_utils import run_bass_kernel_spmd

    a = {k: np.asarray(v) for k, v in inputs.items()}
    arrays = {
        "x": a["x"], "adj": a["adj"],
        "wq0": a["L0_gnn_Wq"], "bq0": a["L0_gnn_bq"].reshape(KD, P).T, "wk0": a["L0_gnn_Wk"], "bk0": a["L0_gnn_bk"].reshape(KD, P).T,
        "wv0": a["L0_gnn_Wv"], "bv0": a["L0_gnn_bv"], "beta": a["L0_gnn_beta"].reshape(1),
        "wq1": a["L1_gnn_Wq"].T, "wk1": a["L1_gnn_Wk"].T, "wv1": a["L1_gnn_Wv"].T, "bv1": a["L1_gnn_bv"],
        "wo1": a["L1_gnn_Wo"].T, "bo1": a["L1_gnn_bo"],
        "ident": np.eye(P, dtype=np.float32),
    }
    arrays = {f"in_{k}": np.ascontiguousarray(v) for k, v in arrays.items()}
    nc = bacc.Bacc("TRN2", target_bir_lowering=False, num_devices=1)
    args = [nc.dram_tensor(k, v.shape, mybir.dt.from_np(v.dtype), kind="ExternalInput").ap() for k, v in arrays.items()]
    args.append(nc.dram_tensor("out_y", (B, N, D), F32, kind="ExternalOutput").ap())
    build(nc, *args)
    r = run_bass_kernel_spmd(nc, [arrays], core_ids=[0])
    return r.results[0]["out_y"]
```

```python
from contextlib import ExitStack, contextmanager

import concourse.bass as bass
from concourse import mybir

F32 = mybir.dt.float32
F32R = mybir.dt.float32r
ALU = mybir.AluOpType
ACT = mybir.ActivationFunctionType

P = 128
B, N, D, H = 8, 1024, 384, 12
HD = D // H
NT = N // P
KD = D // P
HG = P // HD
HALF = 512
GROUPS = B * KD
CHUNK = 256
CHUNKS = N // CHUNK
QT = CHUNK // P
TILES = CHUNKS * HG * QT
CT = HG * QT
INVERT_AT = 3
DIVIDE_AT = 4
TRAIL = 3
SCALAR_COPIES = (0, 2, 4)
BUSY_COPIES = (1, 3, 4)
SIGN_AT = (0, 2)
AHEAD = 3
LATE = 2
SLOTS = GROUPS * CHUNKS + LATE
EPS = 1e-5
MASKED = -9.0e15
BIG = 3.0e38
GONE = -1.0e30
TINY = 1.0e-30


class Scratch:

    def __init__(self, nc):
        self.q = nc.dram_tensor("q_parts", [GROUPS, 2, P, N], F32).ap()
        self.k = nc.dram_tensor("k_parts", [GROUPS, 2, P, N], F32).ap()
        self.v = nc.dram_tensor("v_rows", [GROUPS, P, NT * P], F32).ap()
        self.o = nc.dram_tensor("attended_t", [SLOTS, P, CHUNK], F32).ap()
        self.flags = nc.dram_tensor("maybe_zero_rows", [P, TILES], F32).ap()
        self.x1 = nc.dram_tensor("x_between", [B, N, D], F32).ap()


class Mem:

    def __init__(self, nc, ctx, tag):
        self.nc, self.ctx, self.tag = nc, ctx, tag
        self.holds = self.sem("holds")

    def hold(self, eng, sem, value):
        eng.wait_ge(sem, value)
        eng.sem_inc(self.holds, 1)

    def sb(self, name, shape, dt=F32):
        return self.ctx.enter_context(self.nc.sbuf_tensor(f"{name}_{self.tag}", shape, dt))

    def ps(self, name, shape):
        return self.ctx.enter_context(self.nc.psum_tensor(f"{name}_{self.tag}", shape, F32))

    def sem(self, name):
        return self.ctx.enter_context(self.nc.semaphore(f"{name}_{self.tag}"))


def project(nc, layer, x_in, ident_in, wq_in, wk_in, wv_in, bq_in, bk_in, bv_in, scratch):
    q_scale = float(HD) ** -0.5 if layer == 0 else float(D) ** -0.5
    UNITS = 2 * KD * 2
    ENTRY_SLOTS = UNITS + NT
    MOMENTS_AT = NT
    NORM_AT = NT + 1
    TURN_AT = NT + 3
    LOW_AT = NT + 4
    with ExitStack() as ctx:
        m = Mem(nc, ctx, f"project{layer}")
        ident = m.sb("ident", [P, P])
        w = m.sb("w", [P, 3, KD, D])
        w_parts = m.sb("w_parts", [P, 2, 3, KD, D], F32R)
        qk_bias = m.sb("qk_bias", [P, 2, KD])
        v_bias = m.sb("v_bias", [P, D])
        x = m.sb("x", [P, NT, D])
        h = m.sb("h", [P, NT, D])
        stats = m.sb("stats", [P, NT, 6])
        moments = m.sb("moments", [P, NT, 2])
        var = m.sb("var", [P, NT])
        std = m.sb("std", [P, NT])
        rstd = m.sb("rstd", [P, NT])
        h_t = m.sb("h_t", [P, 2, 2, KD, N], F32R)
        full = m.sb("full", [P, 2, HALF])
        parts = m.sb("parts", [P, 2, 2, N], F32R)
        v_out = m.sb("v_out", [P, 2, KD, NT // 2, P])
        turn_ps = m.ps("turn_ps", [P, 2, HALF])
        qk_ps = m.ps("qk_ps", [P, 2, HALF])
        v_ps = m.ps("v_ps", [P, 2, HALF])

        consts_in = m.sem("consts_in")
        x_loaded = m.sem("x_loaded")
        x_free = m.sem("x_free")
        if layer == 1:
            att = m.sb("att", [P, KD * CHUNKS, CHUNK])
            att_ps = m.ps("att_ps", [P, 2, HALF])
            att_loaded = m.sem("att_loaded")
            att_turned = m.sem("att_turned")
            x_added = m.sem("x_added")
            x1_stored = m.sem("x1_stored")
        stats_done = m.sem("stats_done")
        moments_done = m.sem("moments_done")
        var_ready = m.sem("var_ready")
        std_ready = m.sem("std_ready")
        rstd_ready = m.sem("rstd_ready")
        h_ready = m.sem("h_ready")
        h_turned = m.sem("h_turned")
        h_high_ready = m.sem("h_high_ready")
        h_low_ready = m.sem("h_low_ready")
        qk_done = m.sem("qk_done")
        full_ready = m.sem("full_ready")
        high_ready = m.sem("high_ready")
        low_ready = m.sem("low_ready")
        qk_stored = [m.sem(f"qk_stored{i}") for i in range(2)]
        v_done = m.sem("v_done")
        v_ready = m.sem("v_ready")
        v_stored = [m.sem(f"v_stored{i}") for i in range(2)]
        N_CONSTS = 4 + (3 if layer == 0 else 1)

        block = ctx.enter_context(nc.Block())

        @block.sync
        def _(sp):
            for t, src in enumerate((wq_in, wk_in, wv_in)):
                sp.dma_start(w[:, t], src.rearrange("(c p) n -> p c n", p=P)).then_inc(consts_in, 16)
            sp.dma_start(ident[:], ident_in).then_inc(consts_in, 16)
            sp.dma_start(v_bias[:], bv_in.partition_broadcast(P)).then_inc(consts_in, 16)
            if layer == 0:
                sp.dma_start(qk_bias[:, 0, :], bq_in).then_inc(consts_in, 16)
                sp.dma_start(qk_bias[:, 1, :], bk_in).then_inc(consts_in, 16)
            with sp.Fori(0, B) as b:
                for k in range(UNITS // 2):
                    m.hold(sp, low_ready, b * UNITS + 2 * (k + 1) + 2)
                    sp.dma_start((scratch.q, scratch.k)[k // KD][bass.ds(b * KD + k % KD, 1)].rearrange("a s p n -> p (a s) n"),
                                 parts[:, k % 2].bitcast(F32)).then_inc(qk_stored[k % 2], 16)
                for half in range(2):
                    m.hold(sp, v_ready, b * NT + (half + 1) * (NT // 2))
                    sp.dma_start(scratch.v[bass.ds(b * KD, KD), :, half * HALF:(half + 1) * HALF].rearrange("g p n -> p g n"),
                                 v_out[:, half].rearrange("p g t f -> p g (t f)")).then_inc(v_stored[half], 16)
            for i in range(2):
                sp.wait_ge(qk_stored[i], 16 * (UNITS // 4 * B + 1))
                sp.wait_ge(v_stored[i], 16 * (B + 1))
            if layer == 1:
                sp.wait_ge(x1_stored, 16 * B)

        @block.gpsimd
        def _(pool):
            def load_att(entry):
                pool.dma_start(att[:], scratch.o[bass.ds(entry * (KD * CHUNKS) + LATE, KD * CHUNKS)].rearrange("s p n -> p s n")).then_inc(att_loaded, 16)

            def load_x(entry):
                pool.dma_start(x[:], x_in[bass.ds(entry, 1)].rearrange("a (t p) d -> p (a t) d", p=P)).then_inc(x_loaded, 16)

            def reload(e, entry):
                if layer == 1:
                    pool.wait_ge(x_added, NT * e)
                    pool.dma_start(scratch.x1[bass.ds(e - 1, 1)].rearrange("a (t p) d -> p (a t) d", p=P), x[:]).then_inc(x1_stored, 16)
                    pool.wait_ge(x1_stored, 16 * e)
                    load_att(entry)
                pool.wait_ge(x_free, NT * e)
                load_x(entry)

            for i in range(2):
                pool.nop().then_inc(qk_stored[i], 16)
                pool.nop().then_inc(v_stored[i], 16)
            if layer == 1:
                load_att(0)
            load_x(0)
            with pool.Fori(1, B) as b:
                reload(b, b)
            reload(B, B - 1)

        @block.scalar
        def _(act):
            def deviation(e):
                act.wait_ge(var_ready, e + 1)
                nc.scalar.activation(std[:], var[:], ACT.Sqrt).then_inc(std_ready, 1)

            def relu_high(e, i, t):
                act.wait_ge(h_turned, e * NT + t + 1)
                nc.scalar.activation(h_t[:, i, 0, :, t * P:(t + 1) * P], turn_ps[:, t % 2, 0:D].rearrange("p (c n) -> p c n", c=KD),
                                     ACT.Relu).then_inc(h_high_ready, 1)

            act.wait_ge(consts_in, 16 * N_CONSTS)
            for k in range(3):
                nc.scalar.activation(w_parts[:, 0, k], w[:, k], ACT.Copy)
            deviation(0)
            for t in range(NT):
                relu_high(0, 0, t)
            with act.Fori(0, B, 2) as b0:
                for i in range(2):
                    b = b0 + i
                    for slot in range(ENTRY_SLOTS):
                        if slot < UNITS:
                            k = slot // 2
                            act.wait_ge(full_ready, b * UNITS + slot + 1)
                            act.wait_ge(qk_stored[k % 2], 16 * (b * (UNITS // 4) + k // 2 + 1))
                            nc.scalar.activation(parts[:, k % 2, 0, slot % 2 * HALF:(slot % 2 + 1) * HALF], full[:, slot % 2],
                                                 ACT.Copy).then_inc(high_ready, 1)
                        if slot == MOMENTS_AT:
                            deviation(b + 1)
                        if TURN_AT <= slot < TURN_AT + NT:
                            relu_high(b + 1, 1 - i, slot - TURN_AT)

        @block.vector
        def _(dve):
            def look(e, t):
                if t == 0:
                    dve.wait_ge(x_loaded, 16 * (e + 1))
                if layer == 1:
                    dve.wait_ge(att_turned, e * NT + t + 1)
                    nc.vector.tensor_tensor(x[:, t], x[:, t], att_ps[:, t % 2, 0:D], ALU.add).then_inc(x_added, 1)
                    dve.wait_ge(x_added, e * NT + t + 1)
                nc.vector.bn_stats(stats[:, t], x[:, t]).then_inc(stats_done, 1)

            def variance(e):
                for t in range(NT):
                    m.hold(dve, stats_done, e * NT + t + 1)
                    nc.vector.bn_aggr(moments[:, t], stats[:, t]).then_inc(moments_done, 1)
                dve.wait_ge(moments_done, (e + 1) * NT)
                nc.vector.tensor_scalar(var[:], moments[:, :, 1], EPS, None, ALU.add).then_inc(var_ready, 1)

            def normalise(e, t):
                if t == 0:
                    dve.wait_ge(std_ready, e + 1)
                    nc.vector.reciprocal(rstd[:], std[:]).then_inc(rstd_ready, 1)
                    dve.wait_ge(rstd_ready, e + 1)
                nc.vector.tensor_scalar(h[:, t], x[:, t], moments[:, t, 0:1], rstd[:, t:t + 1], ALU.subtract, ALU.mult).then_inc(h_ready, 1)
                if t == NT - 1:
                    dve.wait_ge(h_ready, (e + 1) * NT)
                    dve.nop().then_inc(x_free, NT)

            def relu_low(e, i, t):
                dve.wait_ge(h_high_ready, e * NT + t + 1)
                nc.vector.scalar_tensor_tensor(h_t[:, i, 1, :, t * P:(t + 1) * P], turn_ps[:, t % 2, 0:D].rearrange("p (c n) -> p c n", c=KD), 0.0,
                                               h_t[:, i, 0, :, t * P:(t + 1) * P].bitcast(F32), ALU.max, ALU.subtract).then_inc(h_low_ready, 1)

            dve.nop().then_inc(low_ready, 2)
            for t in range(NT):
                look(0, t)
            variance(0)
            dve.wait_ge(consts_in, 16 * N_CONSTS)
            for t in range(NT):
                normalise(0, t)
            dve.wait_ge(h_high_ready, 1)
            for k in range(3):
                nc.vector.tensor_tensor(w_parts[:, 1, k], w[:, k], w_parts[:, 0, k].bitcast(F32), ALU.subtract)
            for t in range(NT):
                relu_low(0, 0, t)
            with dve.Fori(0, B, 2) as b0:
                for i in range(2):
                    b = b0 + i
                    for slot in range(ENTRY_SLOTS):
                        if slot < UNITS:
                            u = slot
                            tensor, fg = u // (2 * KD), u // 2 % KD
                            dve.wait_ge(qk_done, b * UNITS + u + 1)
                            dve.wait_ge(low_ready, b * UNITS + u + 1)
                            bias = qk_bias[:, tensor, fg:fg + 1] if layer == 0 else 0.0
                            nc.vector.tensor_scalar(full[:, u % 2], qk_ps[:, u % 2], bias, 1.0 if tensor else q_scale,
                                                    ALU.add, ALU.mult).then_inc(full_ready, 1)
                        else:
                            t = slot - UNITS
                            dve.wait_ge(v_done, b * NT + t + 1)
                            half = t // (NT // 2)
                            if t % (NT // 2) == 0:
                                dve.wait_ge(v_stored[half], 16 * (b + 1))
                            nc.vector.tensor_tensor(v_out[:, half, :, t % (NT // 2)], v_ps[:, t % 2, 0:D].rearrange("p (g f) -> p g f", g=KD),
                                                    v_bias[:].rearrange("p (g f) -> p g f", g=KD), ALU.add).then_inc(v_ready, 1)
                        if slot < NT:
                            look(b + 1, slot)
                        if slot == MOMENTS_AT:
                            variance(b + 1)
                        if NORM_AT <= slot < NORM_AT + NT:
                            normalise(b + 1, slot - NORM_AT)
                        if LOW_AT <= slot < LOW_AT + NT:
                            relu_low(b + 1, 1 - i, slot - LOW_AT)
                        if slot < UNITS:
                            dve.wait_ge(high_ready, b * UNITS + u + 1)
                            half = slice(u % 2 * HALF, (u % 2 + 1) * HALF)
                            nc.vector.tensor_tensor(parts[:, u // 2 % 2, 1, half], full[:, u % 2], parts[:, u // 2 % 2, 0, half].bitcast(F32),
                                                    ALU.subtract).then_inc(low_ready, 1)

        @block.tensor
        def _(pe):
            def turn_att(e, t):
                if t == 0:
                    pe.wait_ge(att_loaded, 16 * (e + 1))
                if t >= 2:
                    pe.wait_ge(x_added, e * NT + t - 1)
                for g in range(KD):
                    last = nc.tensor.transpose(att_ps[:, t % 2, g * P:(g + 1) * P],
                                               att[:, g * CHUNKS + t // QT, (t % QT) * P:(t % QT + 1) * P], ident[:])
                last.then_inc(att_turned, 1)

            def turn_h(e, t):
                pe.wait_ge(h_ready, e * NT + t + 1)
                if t >= 2:
                    pe.wait_ge(h_low_ready, e * NT + t - 1)
                for c in range(KD):
                    last = nc.tensor.transpose(turn_ps[:, t % 2, c * P:(c + 1) * P], h[:, t, c * P:(c + 1) * P], ident[:])
                last.then_inc(h_turned, 1)

            def product(out, stationary, moving):
                passes = [(c, s, v) for c in range(KD) for s, v in ((0, 0), (0, 1), (1, 0))]
                for k, (c, s, v) in enumerate(passes):
                    last = nc.tensor.matmul(out, stationary(s, c), moving(v, c), start=(k == 0), stop=(k == len(passes) - 1))
                return last

            pe.wait_ge(consts_in, 16 * N_CONSTS)
            if layer == 1:
                for t in range(NT):
                    turn_att(0, t)
            for t in range(NT):
                turn_h(0, t)
            with pe.Fori(0, B, 2) as b0:
                for i in range(2):
                    b = b0 + i
                    for slot in range(ENTRY_SLOTS):
                        if slot < UNITS:
                            u = slot
                            tensor, fg, half = u // (2 * KD), u // 2 % KD, u % 2
                            if u < 2:
                                pe.wait_ge(h_low_ready, b * NT + (u + 1) * (NT // 2))
                            else:
                                pe.wait_ge(full_ready, b * UNITS + u - 1)
                            product(qk_ps[:, u % 2], lambda s, c: w_parts[:, s, tensor, c, fg * P:(fg + 1) * P],
                                    lambda v, c: h_t[:, i, v, c, half * HALF:(half + 1) * HALF]).then_inc(qk_done, 1)
                        else:
                            t = slot - UNITS
                            if t >= 2:
                                pe.wait_ge(v_ready, b * NT + t - 1)
                            product(v_ps[:, t % 2, 0:D], lambda s, c: h_t[:, i, s, c, t * P:(t + 1) * P],
                                    lambda v, c: w_parts[:, v, 2, c, :]).then_inc(v_done, 1)
                        if layer == 1 and slot < NT:
                            turn_att(b + 1, slot)
                        if TURN_AT <= slot < TURN_AT + NT:
                            turn_h(b + 1, slot - TURN_AT)


def attend(nc, layer, adj_in, ident_in, beta_in, scratch, guarded=False):
    with ExitStack() as ctx:
        m = Mem(nc, ctx, f"attend{layer}" + "_guarded" * guarded)
        ident = m.sb("ident", [P, P])
        beta = m.sb("beta", [P, 1])
        q_st = m.sb("q_st", [P, HG, N], F32R)
        k_st = m.sb("k_st", [P, HG, N], F32R)
        v_now = m.sb("v_now", [P, NT, P])
        v_kept = m.sb("v_kept", [P, NT, P])
        bias = m.sb("bias", [P, NT, N])
        rows = m.sb("rows", [P, 4, N])
        neg_max = m.sb("neg_max", [P, TILES])
        if layer == 0:
            adj = m.sb("adj", [P, 2, QT, N])
            masked = m.sb("masked", [P, QT, N])
        if layer == 1 and not guarded:
            maybe_zero = m.sb("maybe_zero", [P, TILES])
        if guarded:
            decision = m.sb("decision", [1, 1], mybir.dt.int32)
            spare = m.sb("spare", [P, N])
            neg_min = m.sb("neg_min", [P, TILES])
            max_zero = m.sb("max_zero", [P, TILES])
            all_zero = m.sb("all_zero", [P, TILES])
        shift = m.sb("shift", [P, TILES]) if guarded else neg_max
        probs = m.sb("probs", [P, 2, HG, NT, CHUNK])
        row_sums = m.sb("row_sums", [P, 2, QT, HG])
        inverse = m.sb("inverse", [P, 2, QT, HG])
        divisor = m.sb("divisor", [P, 2, CHUNK])
        inverse_wide = m.sb("inverse_wide", [P, 2, QT, HG, HD])
        out_t = m.sb("out_t", [P, 2, CHUNK])
        s_ps = m.ps("s_ps", [P, 2, N])
        t_ps = m.ps("t_ps", [P, 2, HALF])
        o_ps = m.ps("o_ps", [P, 2, HALF])

        consts_in = m.sem("consts_in")
        inited = m.sem("inited")
        qk_loaded = [m.sem(f"qk_loaded{j}") for j in range(HG)]
        adj_loaded = [m.sem(f"adj_loaded{c}") for c in range(CHUNKS)]
        v_loaded = m.sem("v_loaded")
        v_copied = m.sem("v_copied")
        scored = m.sem("scored")
        negated = m.sem("negated")
        shift_ready = score_read = negated
        if guarded:
            checked = score_read = m.sem("checked")
            max_zero_ready = m.sem("max_zero_ready")
            all_zero_ready = m.sem("all_zero_ready")
            shift_ready = m.sem("shift_ready")
            bounded = m.sem("bounded")
            flags_loaded = m.sem("flags_loaded")
            decided = m.sem("decided")
        elif layer == 1:
            flagged = m.sem("flagged")
            flags_stored = m.sem("flags_stored")
        else:
            positive_ready = m.sem("positive_ready")
            sign_ready = m.sem("sign_ready")
            masked_ready = m.sem("masked_ready")
            bias_ready = m.sem("bias_ready")
        exp_done = m.sem("exp_done")
        low_turned = m.sem("low_turned")
        high_turned = m.sem("high_turned")
        low_copied = m.sem("low_copied")
        high_copied = m.sem("high_copied")
        pv_done = m.sem("pv_done")
        inverted = m.sem("inverted")
        spread = m.sem("spread")
        taken = m.sem("taken")
        out_ready = m.sem("out_ready")
        out_stored = [m.sem(f"out_stored{i}") for i in range(2)]
        QK_IN = 16 * 8
        INITS = 5
        flags = rows[0:1].rearrange("a b n -> a (b n)")[:, 0:P * TILES]

        @contextmanager
        def if_needed(eng):
            if guarded:
                m.hold(eng, decided, 1)
                needed = eng.value_load(decision[0:1, 0:1], min_val=0, max_val=1)
                with eng.If(needed > 0):
                    yield
            else:
                yield

        block = ctx.enter_context(nc.Block())

        def copy(engine_copy, t, half):
            keys = slice(half * NT // 2, (half + 1) * NT // 2)
            return engine_copy(probs[:, t // CT % 2, t // QT % HG, keys, t % QT * P:(t % QT + 1) * P],
                               t_ps[:, half].rearrange("p (k n) -> p k n", k=NT // 2))

        @block.sync
        def _(sp):
            def load_qk(r, j):
                heads = slice(j * HD, (j + 1) * HD)
                for row, part in enumerate((0, 0, 1, 1)):
                    sp.dma_start(q_st[row * HD:(row + 1) * HD, j].bitcast(F32),
                                 scratch.q[bass.ds(r, 1), part, heads, :].rearrange("a p n -> (a p) n")).then_inc(qk_loaded[j], 16)
                for row, part in enumerate((0, 1, 0, 1)):
                    sp.dma_start(k_st[row * HD:(row + 1) * HD, j].bitcast(F32),
                                 scratch.k[bass.ds(r, 1), part, heads, :].rearrange("a p n -> (a p) n")).then_inc(qk_loaded[j], 16)

            def load_adj(b, c, staged=layer == 0):
                dst = adj[:, c % 2] if staged else bias[:, c * QT:(c + 1) * QT]
                sp.dma_start(dst, adj_in[bass.ds(b, 1), c * CHUNK:(c + 1) * CHUNK, :].rearrange("a (t p) n -> p (a t) n", p=P)).then_inc(adj_loaded[c], 16)

            def load_v(r):
                sp.dma_start(v_now[:], scratch.v[bass.ds(r, 1)].rearrange("a p (t f) -> (a p) t f", t=NT)).then_inc(v_loaded, 16)

            def store(n, i):
                m.hold(sp, out_ready, n + 2)
                sp.dma_start(scratch.o[bass.ds(n, 1)].rearrange("a p n -> (a p) n"), out_t[:, i]).then_inc(out_stored[i], 16)

            def stage_adj(this_b, next_b):
                if layer == 0:
                    m.hold(sp, bias_ready, (this_b + 1) * CHUNKS * QT)
                    for c in range(2):
                        load_adj(next_b, c)

            def group(r, next_r, refill):
                for c in range(CHUNKS):
                    if c == CHUNKS - 1:
                        for j in range(HG // 2):
                            m.hold(sp, scored, r * TILES + c * CT + (j + 1) * QT)
                            load_qk(next_r, j)
                    store(r * CHUNKS + c, c % 2)
                    if c == CHUNKS - 1:
                        for j in range(HG // 2, HG):
                            m.hold(sp, scored, r * TILES + c * CT + (j + 1) * QT)
                            load_qk(next_r, j)
                    if refill is not None:
                        this_b, next_b = refill
                        if layer == 1:
                            m.hold(sp, score_read, r * TILES + (c + 1) * CT + guarded)
                            load_adj(next_b, c)
                        elif c < CHUNKS - 2:
                            m.hold(sp, bias_ready, ((this_b + 1) * CHUNKS + c + 1) * QT)
                            load_adj(next_b, c + 2)
                m.hold(sp, pv_done, r * CHUNKS + CHUNKS - 2 + LATE + 1)
                m.hold(sp, v_copied, r + 2)
                load_v(next_r)

            if guarded:
                sp.dma_start(flags, scratch.flags.rearrange("(a p) t -> a (p t)", a=1)).then_inc(flags_loaded, 16)
            with if_needed(sp):
                sp.dma_start(ident[:], ident_in).then_inc(consts_in, 16)
                sp.dma_start(beta[:], beta_in.partition_broadcast(P)).then_inc(consts_in, 16)
                for c in range(CHUNKS):
                    if c == 1:
                        for j in range(HG):
                            load_qk(0, j)
                        load_v(0)
                    load_adj(0, c, staged=False)
                with sp.Fori(0, B - 1) as b:
                    stage_adj(b, b + 1)
                    with sp.Fori(0, KD - 1) as g:
                        group(b * KD + g, b * KD + g + 1, None)
                    group(b * KD + KD - 1, b * KD + KD, (b, b + 1))
                stage_adj(B - 1, B - 1)
                for r in range(GROUPS - KD, GROUPS):
                    group(r, min(r + 1, GROUPS - 1), (B - 1, B - 1) if r == GROUPS - 1 else None)
                for i in range(LATE):
                    store(GROUPS * CHUNKS + i, i)
                for i in range(2):
                    sp.wait_ge(out_stored[i], 16 * (SLOTS // 2 + 1))
                for j in range(HG):
                    sp.wait_ge(qk_loaded[j], QK_IN * (GROUPS + 1))
                for c in range(CHUNKS):
                    sp.wait_ge(adj_loaded[c], 16 * (B + 1))
                sp.wait_ge(v_loaded, 16 * (GROUPS + 1))
                if layer == 1 and not guarded:
                    sp.wait_ge(flagged, GROUPS + 1)
                    sp.dma_start(scratch.flags, maybe_zero[:]).then_inc(flags_stored, 16)
                    sp.wait_ge(flags_stored, 16)

        @block.gpsimd
        def _(pool):
            def positive(b, c, u):
                m.hold(pool, adj_loaded[c], 16 * (b + 1))
                nc.gpsimd.tensor_scalar(adj[:, c % 2, u], adj[:, c % 2, u], 0.0, None, ALU.max).then_inc(positive_ready, 1)

            def mask(b, c, u):
                m.hold(pool, sign_ready, (b * CHUNKS + c) * QT + u + 1)
                nc.gpsimd.tensor_scalar(masked[:, u], masked[:, u], -MASKED, MASKED, ALU.mult, ALU.add).then_inc(masked_ready, 1)

            with if_needed(pool):
                nc.gpsimd.memset(probs[:, 0, :, 0], 1.0).then_inc(inited, 1)
                nc.gpsimd.memset(v_kept[:], 0.0).then_inc(inited, 1)
                nc.gpsimd.memset(row_sums[:, 1], 1.0).then_inc(inited, 1)
                nc.gpsimd.memset(inverse_wide[:, 0], 1.0).then_inc(inited, 1)
                nc.gpsimd.memset(probs[:, 1], 1.0).then_inc(inited, 1)
                for i in range(2):
                    pool.nop().then_inc(out_stored[i], 16)
                if layer == 0:
                    with pool.Fori(1, B + 1) as b:
                        for c in range(CHUNKS + 1):
                            if c:
                                for u in range(QT):
                                    mask(b, c - 1, u)
                            if c < CHUNKS:
                                for u in range(QT):
                                    positive(b, c, u)

        @block.scalar
        def _(act):
            def exp(r, t):
                act.wait_ge(shift_ready, r * TILES + t + 1)
                nc.scalar.activation(rows[:, t % 4], rows[:, t % 4], ACT.Exp, bias=shift[:, t:t + 1], scale=-1.0,
                                     accum_out=row_sums[:, t // CT % 2, t % QT, t // QT % HG:t // QT % HG + 1]).then_inc(exp_done, 1)

            def sign(positives, u, n):
                act.wait_ge(positive_ready, n + 1)
                nc.scalar.activation(masked[:, u], positives, ACT.Sign).then_inc(sign_ready, 1)

            def take(n, i):
                act.wait_ge(pv_done, n + 1)
                act.wait_ge(out_ready, n + 1)
                nc.scalar.activation(divisor[:, i], o_ps[:, i, CHUNK:], ACT.Copy).then_inc(taken, 1)

            def group(r, refill_b):
                for t in range(TILES):
                    c = t // CT
                    exp(r + (t + 1) // TILES, (t + 1) % TILES)
                    if t % CT == 0:
                        act.wait_ge(pv_done, r * CHUNKS + c - 2 + LATE + 1)
                    act.wait_ge(low_turned, r * TILES + t + 1)
                    copy(nc.scalar.copy, t, 0).then_inc(low_copied, 1)
                    if t % CT in (BUSY_COPIES if refill_b is not None and layer == 0 else SCALAR_COPIES):
                        act.wait_ge(high_turned, r * TILES + t + 1 + TRAIL)
                        copy(nc.scalar.copy, t, 1).then_inc(high_copied, 1)
                    if t % CT == 0:
                        take(r * CHUNKS + c, c % 2)
                    if refill_b is not None and layer == 0 and t % CT in SIGN_AT:
                        u = SIGN_AT.index(t % CT)
                        sign(adj[:, c % 2, u], u, (refill_b * CHUNKS + c) * QT + u)

            with if_needed(act):
                act.nop().then_inc(low_copied, 1)
                act.nop().then_inc(exp_done, 1)
                act.wait_ge(inited, INITS)
                if layer == 0:
                    for q in range(NT):
                        act.wait_ge(adj_loaded[q // QT], 16)
                        nc.scalar.activation(bias[:, q], bias[:, q], ACT.Relu).then_inc(positive_ready, 1)
                        if q >= QT:
                            act.wait_ge(bias_ready, q - QT + 1)
                        sign(bias[:, q], q % QT, q)
                exp(0, 0)
                with act.Fori(0, B) as b:
                    with act.Fori(0, KD - 1) as g:
                        group(b * KD + g, None)
                    group(b * KD + KD - 1, b + 1)
                for i in range(LATE):
                    take(GROUPS * CHUNKS + i, i)

        @block.vector
        def _(dve):
            def make_bias(positives, q, n):
                m.hold(dve, masked_ready, n + 1)
                nc.vector.scalar_tensor_tensor(bias[:, q], positives, beta[:, 0:1], masked[:, q % QT],
                                               ALU.mult, ALU.add).then_inc(bias_ready, 1)

            def negate(b, r, t):
                c, qi = t // CT, t // CT * QT + t % QT
                n = r * TILES + t
                if layer == 1 and t % CT == 0:
                    dve.wait_ge(adj_loaded[c], 16 * (b + 1))
                if t == 0 and layer == 1 and not guarded:
                    dve.wait_ge(flagged, r + 1)
                m.hold(dve, scored, n + 1)
                nc.vector.tensor_tensor_reduce(out=rows[:, t % 4], in0=s_ps[:, t % 2], in1=bias[:, qi], scale=-1.0, scalar=BIG,
                                               op0=ALU.add, op1=ALU.min, accum_out=neg_max[:, t:t + 1]).then_inc(negated, 1)
                if guarded:
                    dve.wait_ge(negated, n + 1)
                    m.hold(dve, checked, n + 1)
                    nc.vector.tensor_tensor_reduce(out=spare[:], in0=s_ps[:, t % 2], in1=bias[:, qi], scale=-1.0, scalar=-BIG,
                                                   op0=ALU.add, op1=ALU.max, accum_out=neg_min[:, t:t + 1]).then_inc(checked, 1)
                    nc.vector.tensor_scalar(max_zero[:, t:t + 1], neg_max[:, t:t + 1], 0.0, GONE, ALU.is_equal, ALU.mult).then_inc(max_zero_ready, 1)
                    dve.wait_ge(checked, n + 2)
                    dve.wait_ge(max_zero_ready, n + 1)
                    nc.vector.scalar_tensor_tensor(all_zero[:, t:t + 1], neg_min[:, t:t + 1], 0.0, max_zero[:, t:t + 1],
                                                   ALU.is_equal, ALU.mult).then_inc(all_zero_ready, 1)
                    dve.wait_ge(all_zero_ready, n + 1)
                    nc.vector.tensor_tensor(shift[:, t:t + 1], all_zero[:, t:t + 1], neg_max[:, t:t + 1], ALU.add).then_inc(shift_ready, 1)

            def invert(n, i):
                dve.wait_ge(exp_done, n * CT + 1)
                if guarded:
                    nc.vector.tensor_scalar(row_sums[:, i], row_sums[:, i], TINY, None, ALU.max).then_inc(bounded, 1)
                    dve.wait_ge(bounded, n + 1)
                nc.vector.reciprocal(inverse[:, i], row_sums[:, i]).then_inc(inverted, 1)
                dve.wait_ge(pv_done, n - 2 + LATE + 1)
                dve.wait_ge(inverted, n + 1)
                nc.vector.tensor_copy(inverse_wide[:, i], inverse[:, i].unsqueeze(3).broadcast_to([P, QT, HG, HD])).then_inc(spread, 1)

            def divide(n, n_half, i):
                dve.wait_ge(taken, n + 1)
                dve.wait_ge(out_stored[i], 16 * (n_half + 1))
                nc.vector.tensor_tensor(out_t[:, i], o_ps[:, i, 0:CHUNK], divisor[:, i], ALU.mult).then_inc(out_ready, 1)

            def copy_high(r, t, scalar_copies=SCALAR_COPIES):
                before = (t - TRAIL) % TILES
                if before % CT not in scalar_copies:
                    if before % CT == 1:
                        dve.wait_ge(pv_done, r * CHUNKS + t // CT - 2 + LATE + 1)
                    dve.wait_ge(high_turned, r * TILES + t + 1)
                    copy(nc.vector.tensor_copy, before, 1).then_inc(high_copied, 1)

            def group(b, r, refill_b):
                for t in range(TILES):
                    c = t // CT
                    n = r * TILES + t
                    copy_high(r, t, BUSY_COPIES if refill_b is not None and layer == 0 else SCALAR_COPIES)
                    negate(b, r, t)
                    if t % CT == INVERT_AT:
                        invert(r * CHUNKS + c, (c + 1) % 2)
                    if t % CT == DIVIDE_AT:
                        divide(r * CHUNKS + c, r * (CHUNKS // 2) + c // 2, c % 2)
                    if t == 2 * CT + DIVIDE_AT + 1:
                        dve.wait_ge(v_loaded, 16 * (r + 1))
                        dve.wait_ge(pv_done, r * CHUNKS - 1 + LATE + 1)
                        nc.vector.tensor_copy(v_kept[:], v_now[:]).then_inc(v_copied, 1)
                    if refill_b is not None and layer == 0 and t // QT % HG == HG - 1:
                        dve.wait_ge(negated, n + 1)
                        make_bias(adj[:, c % 2, t % QT], c * QT + t % QT, (refill_b * CHUNKS + c) * QT + t % QT)
                if layer == 1 and not guarded:
                    dve.wait_ge(negated, r * TILES + TILES)
                    nc.vector.scalar_tensor_tensor(maybe_zero[:], neg_max[:], 0.0, maybe_zero[:], ALU.is_equal, ALU.max).then_inc(flagged, 1)

            if guarded:
                dve.wait_ge(flags_loaded, 16)
                nc.vector.reduce_max(decision[:], flags, axis=mybir.AxisListType.X).then_inc(decided, 1)
            with if_needed(dve):
                dve.nop().then_inc(v_copied, 1)
                dve.nop().then_inc(out_ready, 1)
                nc.vector.memset(t_ps[:, 1], 0.0).then_inc(high_turned, TRAIL)
                if guarded:
                    dve.nop().then_inc(checked, 1)
                if layer == 1 and not guarded:
                    nc.vector.memset(maybe_zero[:], 0.0).then_inc(flagged, 1)
                dve.wait_ge(consts_in, 32)
                dve.wait_ge(inited, INITS)
                if layer == 0:
                    for q in range(NT):
                        dve.wait_ge(sign_ready, q + 1)
                        nc.vector.tensor_scalar(masked[:, q % QT], masked[:, q % QT], -MASKED, MASKED, ALU.mult, ALU.add).then_inc(masked_ready, 1)
                        make_bias(bias[:, q], q, q)
                    dve.wait_ge(bias_ready, CHUNKS * QT)
                with dve.Fori(0, B) as b:
                    with dve.Fori(0, KD - 1) as g:
                        group(b, b * KD + g, None)
                    group(b, b * KD + KD - 1, b + 1)
                for t in range(TRAIL):
                    copy_high(GROUPS, t)
                    if t == 0:
                        negate(B, GROUPS, 0)
                invert(GROUPS * CHUNKS, 1)
                for i in range(LATE):
                    divide(GROUPS * CHUNKS + i, GROUPS * CHUNKS // 2, i)

        @block.tensor
        def _(pe):
            def score(t):
                j = t // QT % HG
                queries = slice((t // CT * QT + t % QT) * P, (t // CT * QT + t % QT + 1) * P)
                for half in range(2):
                    last = nc.tensor.matmul(s_ps[:, t % 2, half * HALF:(half + 1) * HALF], q_st[:, j, queries],
                                            k_st[:, j, half * HALF:(half + 1) * HALF], start=True, stop=True)
                last.then_inc(scored, 1)

            def values(i, v, kt):
                for j in range(HG):
                    nc.tensor.matmul(o_ps[j * HD:(j + 1) * HD, i, 0:CHUNK], v[:, kt, j * HD:(j + 1) * HD],
                                     probs[:, i, j, kt], start=(kt == 0), stop=(kt == NT - 1), skip_group_check=True)

            def turn_inverse(i):
                for u in range(QT):
                    last = nc.tensor.transpose(o_ps[:, i, CHUNK + u * P:CHUNK + (u + 1) * P],
                                               inverse_wide[:, i, u].rearrange("p j f -> p (j f)"), ident[:])
                last.then_inc(pv_done, 1)

            with if_needed(pe):
                pe.wait_ge(inited, INITS)
                pe.wait_ge(consts_in, 32)
                values(0, v_kept, 0)
                turn_inverse(0)
                for t in range(AHEAD):
                    if t % QT == 0:
                        pe.wait_ge(qk_loaded[t // QT], QK_IN)
                    if t >= 2:
                        pe.wait_ge(score_read, t - 1 + guarded)
                    score(t)
                with pe.Fori(0, GROUPS) as r:
                    for t in range(TILES):
                        c, kt = t // CT, t % CT
                        n = r * TILES + t
                        ahead = t + AHEAD
                        if ahead % TILES < CT and ahead % QT == 0:
                            pe.wait_ge(qk_loaded[ahead % TILES // QT], QK_IN * (r + 1 + ahead // TILES))
                        pe.wait_ge(score_read, n + AHEAD - 1 + guarded)
                        score(ahead % TILES)
                        pe.wait_ge(exp_done, n + 2)
                        for half, copied, before, turned in ((0, low_copied, 1, low_turned), (1, high_copied, TRAIL, high_turned)):
                            pe.wait_ge(copied, n + before)
                            for k in range(NT // 2):
                                last = nc.tensor.transpose(t_ps[:, half, k * P:(k + 1) * P], rows[:, t % 4, half * HALF + k * P:half * HALF + (k + 1) * P], ident[:])
                            last.then_inc(turned, 1)
                        if kt == 0:
                            pe.wait_ge(low_copied, n + 1)
                            pe.wait_ge(high_copied, n + TRAIL)
                            pe.wait_ge(out_ready, r * CHUNKS + c + 1)
                            if c == 0:
                                pe.wait_ge(v_copied, r + 1)
                            if c == 1:
                                pe.wait_ge(v_loaded, 16 * (r + 1))
                        values((c + 1) % 2, v_now if c else v_kept, kt)
                        if kt == NT - 1:
                            pe.wait_ge(spread, r * CHUNKS + c + 1)
                            turn_inverse((c + 1) % 2)
                pe.wait_ge(low_copied, GROUPS * TILES + 1)
                pe.wait_ge(high_copied, GROUPS * TILES + TRAIL)
                pe.wait_ge(out_ready, GROUPS * CHUNKS + 1)
                pe.wait_ge(v_copied, GROUPS + 1)
                for kt in range(NT):
                    values(1, v_kept, kt)
                pe.wait_ge(spread, GROUPS * CHUNKS + 1)
                turn_inverse(1)


def finish(nc, wo_in, bo_in, scratch, out):
    with ExitStack() as ctx:
        m = Mem(nc, ctx, "finish")
        w = m.sb("w", [P, KD, D])
        w_parts = m.sb("w_parts", [P, 2, KD, D], F32R)
        bo = m.sb("bo", [P, D])
        x = m.sb("x", [P, 2, NT, D])
        att = m.sb("att", [P, 2, KD, CHUNKS, CHUNK])
        att_parts = m.sb("att_parts", [P, 2, 2, KD, CHUNKS, CHUNK], F32R)
        y_ps = m.ps("y_ps", [P, 4, HALF])
        consts_in = m.sem("consts_in")
        att_loaded = [m.sem(f"att_loaded{i}") for i in range(2)]
        x_loaded = [m.sem(f"x_loaded{i}") for i in range(2)]
        att_high_ready = m.sem("att_high_ready")
        att_low_ready = m.sem("att_low_ready")
        biased = m.sem("biased")
        multiplied = m.sem("multiplied")
        added = m.sem("added")
        stored = [m.sem(f"stored{i}") for i in range(2)]
        block = ctx.enter_context(nc.Block())

        @block.sync
        def _(sp):
            def load_att(b, i):
                sp.dma_start(att[:, i].rearrange("p g c n -> p (g c) n"),
                             scratch.o[bass.ds(b * (KD * CHUNKS) + LATE, KD * CHUNKS)].rearrange("s p n -> p s n")).then_inc(att_loaded[i], 16)

            def load_x(b, i):
                sp.dma_start(x[:, i], scratch.x1[bass.ds(b, 1)].rearrange("a (t p) d -> p (a t) d", p=P)).then_inc(x_loaded[i], 16)

            def store(b, i):
                for t in (NT // 2, NT):
                    rows = slice((t - NT // 2) * P, t * P)
                    m.hold(sp, added, b * NT + t + 4)
                    sp.dma_start(out[bass.ds(b, 1), rows].rearrange("a (t p) d -> p (a t) d", p=P), x[:, i, t - NT // 2:t]).then_inc(stored[i], 16)

            load_att(0, 0)
            sp.dma_start(w[:], wo_in.rearrange("(c p) n -> p c n", p=P)).then_inc(consts_in, 16)
            sp.dma_start(bo[:], bo_in.partition_broadcast(P)).then_inc(consts_in, 16)
            load_x(0, 0)
            load_att(1, 1)
            load_x(1, 1)
            with sp.Fori(0, B // 2 - 1) as pair:
                for i in range(2):
                    b = 2 * pair + i
                    m.hold(sp, att_low_ready, (b + 1) * CHUNKS)
                    load_att(b + 2, i)
                    store(b, i)
                    m.hold(sp, stored[i], 32 * (pair + 1))
                    load_x(b + 2, i)
            for i in range(2):
                store(B - 2 + i, i)
            for i in range(2):
                sp.wait_ge(stored[i], 32 * (B // 2))

        @block.gpsimd
        def _(pool):
            pool.nop().then_inc(multiplied, 2 * NT)
            pool.nop().then_inc(added, 4)
            pool.wait_ge(consts_in, 32)
            with pool.Fori(0, B, 2) as b0:
                for i in range(2):
                    m.hold(pool, x_loaded[i], 16 * (b0 // 2 + 1))
                    for t in range(NT):
                        nc.gpsimd.tensor_tensor(x[:, i, t], x[:, i, t], bo[:], ALU.add).then_inc(biased, 1)

        @block.scalar
        def _(act):
            act.wait_ge(consts_in, 32)
            nc.scalar.activation(w_parts[:, 0], w[:], ACT.Copy)
            with act.Fori(0, B, 2) as b0:
                for i in range(2):
                    b = b0 + i
                    act.wait_ge(att_loaded[i], 16 * (b0 // 2 + 1))
                    for c in range(CHUNKS):
                        act.wait_ge(multiplied, b * NT + (c + 1) * QT)
                        nc.scalar.activation(att_parts[:, i, 0, :, c], att[:, i, :, c], ACT.Copy).then_inc(att_high_ready, 1)

        @block.vector
        def _(dve):
            def low_part(b, i, c):
                dve.wait_ge(att_high_ready, b * CHUNKS + c + 1)
                nc.vector.tensor_tensor(att_parts[:, i, 1, :, c], att[:, i, :, c], att_parts[:, i, 0, :, c].bitcast(F32),
                                        ALU.subtract).then_inc(att_low_ready, 1)

            dve.wait_ge(att_high_ready, 1)
            nc.vector.tensor_tensor(w_parts[:, 1], w[:], w_parts[:, 0].bitcast(F32), ALU.subtract)
            def entry(b, i, last):
                for t in range(NT):
                    n = b * NT + t
                    c = t // QT + 2
                    if t % QT == 0 and c < CHUNKS:
                        low_part(b, i, c)
                    elif t % QT == 0 and not last:
                        low_part(b + 1, 1 - i, c - CHUNKS)
                    dve.wait_ge(multiplied, n + 1 + 2 * NT)
                    dve.wait_ge(biased, n + 1)
                    nc.vector.tensor_tensor(x[:, i, t], x[:, i, t], y_ps[:, t % 4, 0:D], ALU.add).then_inc(added, 1)

            for c in range(2):
                low_part(0, 0, c)
            with dve.Fori(0, B - 2, 2) as b0:
                for i in range(2):
                    entry(b0 + i, i, False)
            for i in range(2):
                entry(B - 2 + i, i, i == 1)

        @block.tensor
        def _(pe):
            with pe.Fori(0, B, 2) as b0:
                for i in range(2):
                    b = b0 + i
                    for t in range(NT):
                        c, u = t // QT, t % QT
                        if u == 0:
                            pe.wait_ge(att_low_ready, b * CHUNKS + c + 1)
                        pe.wait_ge(added, b * NT + t + 1)
                        passes = [(g, s, v) for g in range(KD) for s, v in ((0, 0), (0, 1), (1, 0))]
                        for k, (g, s, v) in enumerate(passes):
                            last = nc.tensor.matmul(y_ps[:, t % 4, 0:D], att_parts[:, i, s, g, c, u * P:(u + 1) * P], w_parts[:, v, g, :],
                                                    start=(k == 0), stop=(k == len(passes) - 1))
                        last.then_inc(multiplied, 1)


def build(nc, x, adj, wq0, bq0, wk0, bk0, wv0, bv0, beta, wq1, wk1, wv1, bv1, wo1, bo1, ident, out):
    scratch = Scratch(nc)
    project(nc, 0, x, ident, wq0, wk0, wv0, bq0, bk0, bv0, scratch)
    attend(nc, 0, adj, ident, beta, scratch)
    project(nc, 1, x, ident, wq1, wk1, wv1, None, None, bv1, scratch)
    attend(nc, 1, adj, ident, beta, scratch)
    attend(nc, 1, adj, ident, beta, scratch, guarded=True)
    finish(nc, wo1, bo1, scratch, out)


def kernel(**inputs):
    import numpy as np
    import concourse.bacc as bacc
    from concourse.bass_utils import run_bass_kernel_spmd

    a = {k: np.asarray(v) for k, v in inputs.items()}
    arrays = {
        "x": a["x"], "adj": a["adj"],
        "wq0": a["L0_gnn_Wq"], "bq0": a["L0_gnn_bq"].reshape(KD, P).T, "wk0": a["L0_gnn_Wk"], "bk0": a["L0_gnn_bk"].reshape(KD, P).T,
        "wv0": a["L0_gnn_Wv"], "bv0": a["L0_gnn_bv"], "beta": a["L0_gnn_beta"].reshape(1),
        "wq1": a["L1_gnn_Wq"].T, "wk1": a["L1_gnn_Wk"].T, "wv1": a["L1_gnn_Wv"].T, "bv1": a["L1_gnn_bv"],
        "wo1": a["L1_gnn_Wo"].T, "bo1": a["L1_gnn_bo"],
        "ident": np.eye(P, dtype=np.float32),
    }
    arrays = {f"in_{k}": np.ascontiguousarray(v) for k, v in arrays.items()}
    nc = bacc.Bacc("TRN2", target_bir_lowering=False, num_devices=1)
    args = [nc.dram_tensor(k, v.shape, mybir.dt.from_np(v.dtype), kind="ExternalInput").ap() for k, v in arrays.items()]
    args.append(nc.dram_tensor("out_y", (B, N, D), F32, kind="ExternalOutput").ap())
    build(nc, *args)
    r = run_bass_kernel_spmd(nc, [arrays], core_ids=[0])
    return r.results[0]["out_y"]
```
